# Optimizing a Trainium2 kernel written in Bass

```python
import numpy as np
import jax
import jax.numpy as jnp

def _softmax(x, axis=-1):
    return jax.nn.softmax(x, axis=axis)

def _gelu(x):
    return jax.nn.gelu(x, approximate=True)

def _silu(x):
    return jax.nn.silu(x)

def _sigmoid(x):
    return jax.nn.sigmoid(x)

def _layernorm(x, axis=-1, eps=1e-05):
    m = jnp.mean(x, axis=axis, keepdims=True)
    v = jnp.var(x, axis=axis, keepdims=True)
    return (x - m) / jnp.sqrt(v + eps)

def _scatter_add(tgt, idx, src, axis=0):
    return tgt.at[idx].add(src)

def _segment_sum(src, seg, n):
    return jax.ops.segment_sum(src, seg, n)
kernel_name = 'mk_decoder_postln_d1_seqx_r2_d0452f'

def setup_inputs(seed: int=0):
    np.random.seed(seed)
    _w = jnp.asarray

    def _rec_inputs():
        import jax
        import jax.numpy as jnp
        _rk = jax.random.key(seed)
        x = -0.0002928 + 1 * jax.random.normal(jax.random.fold_in(_rk, 1), (2, 2048, 512), jnp.float32)
        _lenS = 2048 - jax.random.randint(jax.random.fold_in(_rk, 7), (2,), 0, max(1, 2048 // 4) + 1, jnp.int32)
        _lenS2 = 77 - jax.random.randint(jax.random.fold_in(_rk, 8), (2,), 0, max(1, 77 // 4) + 1, jnp.int32)
        _ctx_1024P = jax.random.normal(jax.random.fold_in(_rk, 11), (2, 16, 512), jnp.float32)
        _ctx_1024c = jax.random.dirichlet(jax.random.fold_in(_rk, 511), 0.3 * jnp.ones((16,), jnp.float32), (2, 77))
        _ctx_1024t = jnp.einsum('bsk,bkd->bsd', _ctx_1024c, _ctx_1024P)
        _ctx_1024t = _ctx_1024t * jax.lax.rsqrt(jnp.mean(jnp.square(_ctx_1024t)) + 1e-12) * 0.953939
        ctx_1024 = -1.39393e-06 + 0.999914 * (_ctx_1024t + 0.3 * jax.random.normal(jax.random.fold_in(_rk, 611), (2, 77, 512), jnp.float32))
        _validS = jnp.arange(2048)[None, :] < _lenS[:, None]
        _validS2 = jnp.arange(77)[None, :] < _lenS2[:, None]
        _causal = jnp.tril(jnp.ones((2048, 2048), dtype=bool))
        mask_1x1xSxS2_ik0 = jnp.where(jnp.broadcast_to(_validS2[0:1, None, None, :], (1, 1, 2048, 77)), 0, 1).astype(jnp.int32)
        return (x, ctx_1024, mask_1x1xSxS2_ik0)
    x, ctx_1024, mask_1x1xSxS2_ik0 = _rec_inputs()

    def _L0_attn_setup():
        import jax, jax.numpy as jnp
        import numpy as np
        D_MODEL, D_INNER, D_STATE = (512, 1024, 16)
        BATCH, SEQ = (4, 1024)

        def silu(x):
            return x * jax.nn.sigmoid(x)

        def selective_scan(u, delta, A, B, C, D):
            bsz = u.shape[0]

            def step(h, xs):
                u_t, dt_t, B_t, C_t = xs
                dA = jnp.exp(dt_t[..., None] * A)
                dBu = (dt_t * u_t)[..., None] * B_t[:, None, :]
                h = h * dA + dBu
                y_t = jnp.einsum('bds,bs->bd', h, C_t) + D * u_t
                return (h, y_t)
            h0 = jnp.zeros((bsz, u.shape[2], A.shape[1]), u.dtype)
            xs = (u.swapaxes(0, 1), delta.swapaxes(0, 1), B.swapaxes(0, 1), C.swapaxes(0, 1))
            _, ys = jax.lax.scan(step, h0, xs)
            return ys.swapaxes(0, 1)
        key = jax.random.key(seed)
        ks = jax.random.split(key, 11)
        s_in = 1.0 / np.sqrt(D_MODEL)
        s_inner = 1.0 / np.sqrt(D_INNER)
        return {'x': jax.random.normal(ks[0], (BATCH, SEQ, D_MODEL), jnp.float32), 'W_in': jax.random.normal(ks[1], (D_MODEL, 2 * D_INNER), jnp.float32) * s_in, 'b_in': jax.random.normal(ks[2], (2 * D_INNER,), jnp.float32) * s_in, 'W_xproj': jax.random.normal(ks[3], (D_INNER, 2 * D_STATE), jnp.float32) * s_inner, 'b_xproj': jax.random.normal(ks[4], (2 * D_STATE,), jnp.float32) * s_inner, 'W_dt': jax.random.normal(ks[5], (D_INNER, D_INNER), jnp.float32) * s_inner, 'b_dt': jax.random.normal(ks[6], (D_INNER,), jnp.float32) * s_inner, 'W_out': jax.random.normal(ks[7], (D_INNER, D_MODEL), jnp.float32) * s_inner, 'b_out': jax.random.normal(ks[8], (D_MODEL,), jnp.float32) * s_inner, 'A_log': jax.random.uniform(ks[9], (D_INNER, D_STATE), jnp.float32, 0.0, np.log(16.0)), 'D_param': jnp.ones((D_INNER,), jnp.float32)}
    _L0_attn_all = _L0_attn_setup()
    _L0_attn_in = {k: v for k, v in _L0_attn_all.items() if k in ('W_in', 'b_in', 'W_xproj', 'b_xproj', 'W_dt', 'b_dt', 'W_out', 'b_out', 'A_log', 'D_param')}
    del _L0_attn_all

    def _L0_xattn_setup():
        import jax, jax.numpy as jnp
        import numpy as np
        B, S, D, H = (2, 1024, 512, 16)
        DK = D // H

        def _split_heads(x):
            b, s, d = x.shape
            return x.reshape(b, s, H, DK).transpose(0, 2, 1, 3)
        key = jax.random.key(seed)
        ks = jax.random.split(key, 12)
        sc = 1.0 / np.sqrt(D)
        inp = {'q': jax.random.normal(ks[0], (B, S, D), jnp.float32), 'k': jax.random.normal(ks[1], (B, S, D), jnp.float32), 'v': jax.random.normal(ks[2], (B, S, D), jnp.float32), 'wq_w': jax.random.normal(ks[3], (D, D), jnp.float32) * sc, 'wq_b': jax.random.normal(ks[4], (D,), jnp.float32) * sc, 'wk_w': jax.random.normal(ks[5], (D, D), jnp.float32) * sc, 'wk_b': jax.random.normal(ks[6], (D,), jnp.float32) * sc, 'wv_w': jax.random.normal(ks[7], (D, D), jnp.float32) * sc, 'wv_b': jax.random.normal(ks[8], (D,), jnp.float32) * sc, 'wo_w': jax.random.normal(ks[9], (D, D), jnp.float32) * sc, 'wo_b': jax.random.normal(ks[10], (D,), jnp.float32) * sc, 'mask': jnp.tril(jnp.ones((S, S), jnp.int32))[None, None, :, :]}
        return inp
    _L0_xattn_all = _L0_xattn_setup()
    _L0_xattn_in = {k: v for k, v in _L0_xattn_all.items() if k in ('wq_w', 'wq_b', 'wk_w', 'wk_b', 'wv_w', 'wv_b', 'wo_w', 'wo_b')}
    del _L0_xattn_all

    def _L0_ffn_setup():
        import jax, jax.numpy as jnp
        import numpy as np
        B, S, D_MODEL, D_FF = (4, 1024, 512, 2048)

        def _quantum_transform(hidden, theta, w_real, w_imag):
            imag = w_imag * jnp.sin(theta + hidden * 0.1)
            quantum_phase = jnp.cos(theta) * w_real + jnp.sin(theta) * w_imag
            return hidden + quantum_phase * imag * 0.1
        key = jax.random.key(seed)
        ks = jax.random.split(key, 8)
        return {'x': jax.random.normal(ks[0], (B, S, D_MODEL), dtype=jnp.float32), 'W1': jax.random.normal(ks[1], (D_MODEL, D_FF), dtype=jnp.float32) * (1.0 / np.sqrt(D_MODEL)), 'b1': jnp.zeros((D_FF,), dtype=jnp.float32), 'quantum_phases': jax.random.normal(ks[2], (D_FF,), dtype=jnp.float32) * (2.0 * np.pi), 'quantum_weights_real': jax.random.normal(ks[3], (D_FF,), dtype=jnp.float32) * 0.1, 'quantum_weights_imag': jax.random.normal(ks[4], (D_FF,), dtype=jnp.float32) * 0.1, 'W2': jax.random.normal(ks[5], (D_FF, D_MODEL), dtype=jnp.float32) * (1.0 / np.sqrt(D_FF)), 'b2': jnp.zeros((D_MODEL,), dtype=jnp.float32)}
    _L0_ffn_all = _L0_ffn_setup()
    _L0_ffn_in = {k: v for k, v in _L0_ffn_all.items() if k in ('W1', 'b1', 'quantum_phases', 'quantum_weights_real', 'quantum_weights_imag', 'W2', 'b2')}
    del _L0_ffn_all
    return {'x': x, 'ctx_1024': ctx_1024, 'mask_1x1xSxS2_ik0': mask_1x1xSxS2_ik0, 'L0_attn_W_in': _L0_attn_in['W_in'], 'L0_attn_b_in': _L0_attn_in['b_in'], 'L0_attn_W_xproj': _L0_attn_in['W_xproj'], 'L0_attn_b_xproj': _L0_attn_in['b_xproj'], 'L0_attn_W_dt': _L0_attn_in['W_dt'], 'L0_attn_b_dt': _L0_attn_in['b_dt'], 'L0_attn_W_out': _L0_attn_in['W_out'], 'L0_attn_b_out': _L0_attn_in['b_out'], 'L0_attn_A_log': _L0_attn_in['A_log'], 'L0_attn_D_param': _L0_attn_in['D_param'], 'L0_xattn_wq_w': _L0_xattn_in['wq_w'], 'L0_xattn_wq_b': _L0_xattn_in['wq_b'], 'L0_xattn_wk_w': _L0_xattn_in['wk_w'], 'L0_xattn_wk_b': _L0_xattn_in['wk_b'], 'L0_xattn_wv_w': _L0_xattn_in['wv_w'], 'L0_xattn_wv_b': _L0_xattn_in['wv_b'], 'L0_xattn_wo_w': _L0_xattn_in['wo_w'], 'L0_xattn_wo_b': _L0_xattn_in['wo_b'], 'L0_ffn_W1': _L0_ffn_in['W1'], 'L0_ffn_b1': _L0_ffn_in['b1'], 'L0_ffn_quantum_phases': _L0_ffn_in['quantum_phases'], 'L0_ffn_quantum_weights_real': _L0_ffn_in['quantum_weights_real'], 'L0_ffn_quantum_weights_imag': _L0_ffn_in['quantum_weights_imag'], 'L0_ffn_W2': _L0_ffn_in['W2'], 'L0_ffn_b2': _L0_ffn_in['b2']}

def reference(x, ctx_1024, mask_1x1xSxS2_ik0, L0_attn_W_in, L0_attn_b_in, L0_attn_W_xproj, L0_attn_b_xproj, L0_attn_W_dt, L0_attn_b_dt, L0_attn_W_out, L0_attn_b_out, L0_attn_A_log, L0_attn_D_param, L0_xattn_wq_w, L0_xattn_wq_b, L0_xattn_wk_w, L0_xattn_wk_b, L0_xattn_wv_w, L0_xattn_wv_b, L0_xattn_wo_w, L0_xattn_wo_b, L0_ffn_W1, L0_ffn_b1, L0_ffn_quantum_phases, L0_ffn_quantum_weights_real, L0_ffn_quantum_weights_imag, L0_ffn_W2, L0_ffn_b2):
    import jax
    import jax.numpy as jnp

    def _L0_attn_ref(x, W_in, b_in, W_xproj, b_xproj, W_dt, b_dt, W_out, b_out, A_log, D_param):
        import jax, jax.numpy as jnp
        import numpy as np
        D_MODEL, D_INNER, D_STATE = (512, 1024, 16)
        BATCH, SEQ = (4, 1024)

        def silu(x):
            return x * jax.nn.sigmoid(x)

        def selective_scan(u, delta, A, B, C, D):
            bsz = u.shape[0]

            def step(h, xs):
                u_t, dt_t, B_t, C_t = xs
                dA = jnp.exp(dt_t[..., None] * A)
                dBu = (dt_t * u_t)[..., None] * B_t[:, None, :]
                h = h * dA + dBu
                y_t = jnp.einsum('bds,bs->bd', h, C_t) + D * u_t
                return (h, y_t)
            h0 = jnp.zeros((bsz, u.shape[2], A.shape[1]), u.dtype)
            xs = (u.swapaxes(0, 1), delta.swapaxes(0, 1), B.swapaxes(0, 1), C.swapaxes(0, 1))
            _, ys = jax.lax.scan(step, h0, xs)
            return ys.swapaxes(0, 1)
        xz = x @ W_in + b_in
        x_proj, z = jnp.split(xz, 2, axis=-1)
        x_conv = silu(x_proj)
        A = -jnp.exp(A_log)
        x_dbl = x_conv @ W_xproj + b_xproj
        B, C = jnp.split(x_dbl, 2, axis=-1)
        dt = jax.nn.softplus(x_conv @ W_dt + b_dt)
        y = selective_scan(x_conv, dt, A, B, C, D_param)
        y = y * silu(z)
        return y @ W_out + b_out

    def _L0_xattn_ref(q, k, v, wq_w, wq_b, wk_w, wk_b, wv_w, wv_b, wo_w, wo_b, mask):
        import jax, jax.numpy as jnp
        import numpy as np
        B, S, D, H = (2, 1024, 512, 16)
        DK = D // H

        def _split_heads(x):
            b, s, d = x.shape
            return x.reshape(b, s, H, DK).transpose(0, 2, 1, 3)
        qh = _split_heads(q @ wq_w.T + wq_b)
        kh = _split_heads(k @ wk_w.T + wk_b)
        vh = _split_heads(v @ wv_w.T + wv_b)
        scores = jnp.einsum('bhsk,bhtk->bhst', qh, kh) / np.sqrt(DK).astype(np.float32)
        scores = jnp.where(mask == 0, jnp.float32(-1000000000.0), scores)
        probs = jax.nn.softmax(scores, axis=-1)
        attn = jnp.einsum('bhst,bhtk->bhsk', probs, vh)
        out = attn.transpose(0, 2, 1, 3).reshape(q.shape[0], q.shape[1], D)
        return out @ wo_w.T + wo_b

    def _L0_ffn_ref(x, W1, b1, quantum_phases, quantum_weights_real, quantum_weights_imag, W2, b2):
        import jax, jax.numpy as jnp
        import numpy as np
        B, S, D_MODEL, D_FF = (4, 1024, 512, 2048)

        def _quantum_transform(hidden, theta, w_real, w_imag):
            imag = w_imag * jnp.sin(theta + hidden * 0.1)
            quantum_phase = jnp.cos(theta) * w_real + jnp.sin(theta) * w_imag
            return hidden + quantum_phase * imag * 0.1
        hidden = jnp.einsum('bsd,df->bsf', x, W1) + b1
        q = _quantum_transform(hidden, quantum_phases, quantum_weights_real, quantum_weights_imag)
        act = jax.nn.relu(q)
        return jnp.einsum('bsf,fd->bsd', act, W2) + b2
    x = _layernorm(x + _L0_attn_ref(x, L0_attn_W_in, L0_attn_b_in, L0_attn_W_xproj, L0_attn_b_xproj, L0_attn_W_dt, L0_attn_b_dt, L0_attn_W_out, L0_attn_b_out, L0_attn_A_log, L0_attn_D_param), axis=-1)
    x = _layernorm(x + _L0_xattn_ref(x, ctx_1024, ctx_1024, L0_xattn_wq_w, L0_xattn_wq_b, L0_xattn_wk_w, L0_xattn_wk_b, L0_xattn_wv_w, L0_xattn_wv_b, L0_xattn_wo_w, L0_xattn_wo_b, mask_1x1xSxS2_ik0), axis=-1)
    x = _layernorm(x + _L0_ffn_ref(x, L0_ffn_W1, L0_ffn_b1, L0_ffn_quantum_phases, L0_ffn_quantum_weights_real, L0_ffn_quantum_weights_imag, L0_ffn_W2, L0_ffn_b2), axis=-1)
    return x

_drawn_inputs = setup_inputs


def setup_inputs(seed=0):
    import zlib

    import numpy as np

    out = dict(_drawn_inputs(seed))
    spreads = {'L0_attn_D_param': (1.0, 0.2), 'L0_ffn_b1': (0.0, 0.1), 'L0_ffn_b2': (0.0, 0.1)}
    factors = {'L0_attn_b_xproj': 3.161,
     'L0_attn_b_dt': 8.0,
     'L0_xattn_wq_b': 6.898,
     'L0_xattn_wk_b': 200.0,
     'L0_ffn_quantum_phases': 8.0,
     'L0_ffn_quantum_weights_real': 37.901,
     'L0_ffn_quantum_weights_imag': 8.0,
     'L0_attn_b_out': 2.668}
    for name, (base, spread) in spreads.items():
        noise = np.random.default_rng([zlib.crc32(name.encode()), seed]).standard_normal(out[name].shape)
        drawn = base * np.exp(spread * noise) if base else spread * noise
        out[name] = jnp.asarray(drawn.astype(out[name].dtype))
    for name, factor in factors.items():
        out[name] = (out[name] * factor).astype(out[name].dtype)
    return out
```

```python
import math
from contextlib import ExitStack

import concourse.bass as bass
from concourse import mybir

FP32 = mybir.dt.float32
FP16 = mybir.dt.float16
INT32 = mybir.dt.int32
ALU = mybir.AluOpType
ACT = mybir.ActivationFunctionType
AXIS_X = mybir.AxisListType.X

P = 128
BATCH, SEQ, D = 2, 2048, 512
TOKENS = BATCH * SEQ
KD = D // P
INNER, NSTATE = 1024, 16
NJ = INNER // P
CTX = 77
HEADS = 16
DK = D // HEADS
FF = 2048
NF = FF // P
TC = 256
CHUNKS = TOKENS // TC
PER_BATCH = CHUNKS // BATCH
EPS = 1e-5
W_SCALE = 64.0
UNSCALE = 1.0 / W_SCALE



def split_product(nc, out, w, x, start, stop):
    nc.tensor.matmul(out, w[0], x[0], start=start, stop=False)
    nc.tensor.matmul(out, w[0], x[1], start=False, stop=False)
    return nc.tensor.matmul(out, w[1], x[0], start=False, stop=stop)


GS = 4
NG = NSTATE // GS
GROUPS = NJ * NG
RING = 4


def selective_scan_phase(nc, a):
    with ExitStack() as ctx:
        def sb(name, shape, dt=FP32):
            return ctx.enter_context(nc.sbuf_tensor(name, shape, dt))

        def sem(name):
            return ctx.enter_context(nc.semaphore(name))

        w_in = [sb(f"w_in_{n}", [P, KD, 2 * INNER], FP16) for n in ("high", "low")]
        w_xp32 = sb("w_xp32", [P, NJ, 2 * NSTATE])
        w_xp = [sb(f"w_xp_{n}", [P, NJ, 2 * NSTATE], FP16) for n in ("high", "low")]
        w_dt = [sb(f"w_dt_{n}", [P, NJ, INNER], FP16) for n in ("high", "low")]
        b_in = sb("b_in", [P, 2 * NJ])
        b_dt = sb("b_dt", [P, NJ])
        b_dt64 = sb("b_dt64", [P, NJ])
        b_xp = sb("b_xp", [2 * NSTATE, 1])
        d_skip = sb("d_skip", [P, NJ])
        decay = sb("decay", [P, NJ, NSTATE])
        x_t = sb("x_t", [P, KD, TC])
        x16 = [sb(f"x_{n}", [P, 2, KD, TC], FP16) for n in ("high", "low")]
        u16 = [sb(f"u_{n}", [P, NJ, TC], FP16) for n in ("high", "low")]
        u = sb("u", [P, 2, NJ, TC])
        z = sb("z", [P, NJ, TC])
        dt = sb("dt", [P, NJ, TC])
        soft = sb("soft", [P, 4, TC])
        dtu = sb("dtu", [P, 2, TC])
        bc = sb("bc", [2 * NSTATE, TC])
        b_rep = sb("b_rep", [P, NSTATE, TC])
        c_rep = sb("c_rep", [P, NSTATE, TC])
        da = sb("da", [P, RING, GS, TC])
        h = sb("h", [P, RING, GS, TC])
        h_last = sb("h_last", [P, NJ, NSTATE])
        zeros = sb("zeros", [P, GS])
        y = sb("y", [P, 2, TC])

        proj = ctx.enter_context(nc.psum_tensor("proj", [P, NJ, TC], FP32))
        bc_ps = ctx.enter_context(nc.psum_tensor("bc_ps", [2 * NSTATE, 512], FP32))
        y_ps = ctx.enter_context(nc.psum_tensor("y_ps", [P, 2, 512], FP32))

        s_w = [sem(f"a_weights_{n}_loaded") for n in range(4)]
        s_wh, s_wl = sem("a_weights_high"), sem("a_weights_low")
        s_small = sem("a_small_loaded")
        s_xh, s_xl, s_uh, s_ul = sem("a_x_high"), sem("a_x_low"), sem("a_u_high"), sem("a_u_low")
        s_x = sem("a_x_loaded")
        s_const = sem("a_decay_ready")
        s_up, s_zp, s_bcp, s_dtp = sem("a_u_psum"), sem("a_z_psum"), sem("a_bc_psum"), sem("a_dt_psum")
        s_u, s_z, s_bc = sem("a_u_ready"), sem("a_z_ready"), sem("a_bc_ready")
        s_abs, s_relu = sem("a_abs_done"), sem("a_relu_done")
        s_sexp, s_soft, s_dt = sem("a_soft_exp_done"), sem("a_soft_ready"), sem("a_dt_ready")
        s_bcd = sem("a_bc_in_dram")
        s_b = [sem(f"a_b_rep_{g}") for g in range(NG)]
        s_c = [sem(f"a_c_rep_{g}") for g in range(NG)]
        s_dtu = sem("a_dtu_ready")
        s_dbu = sem("a_dbu_ready")
        s_da = sem("a_da_ready")
        s_scan = sem("a_scanned")
        s_hz, s_hl = sem("a_h_last_cleared"), sem("a_h_last_saved")
        s_hc = sem("a_hc_ready")
        s_sum = sem("a_summed")
        s_gate = sem("a_skip_added")
        s_y = sem("a_y_ready")
        s_yout = [sem("a_y_stored_even"), sem("a_y_stored_odd")]

        DBU_CREDIT, SCAN_CREDIT, SUM_CREDIT, GATE_CREDIT, Y_CREDIT, STORE_CREDIT = 2 * NG, RING, RING, 2, 1, 16

        block = ctx.enter_context(nc.Block())

        pieces = []
        for n in range(4):
            stage = (h if n % 2 == 0 else da)[:, :, :, :].rearrange("p r s t -> p (r s t)")
            if n < 2:
                where = (slice(None), slice(None), slice(n * INNER, (n + 1) * INNER))
                pieces.append((stage.rearrange("p (k n) -> p k n", k=KD),
                               a["w_in"].rearrange("(k p) n -> p k n", p=P)[where],
                               w_in[0][where], w_in[1][where]))
            else:
                where = (slice(None), slice((n - 2) * NJ // 2, (n - 1) * NJ // 2), slice(None))
                pieces.append((stage.rearrange("p (k n) -> p k n", k=NJ // 2),
                               a["w_dt"].rearrange("(k p) n -> p k n", p=P)[where],
                               w_dt[0][where], w_dt[1][where]))

        def all_chunks(e, main, between=None):
            half = PER_BATCH // 2
            for p in range(2):
                main(p, p, False)
            with e.Fori(1, half) as i:
                for p in range(2):
                    main(i * 2 + p, p, False)
            if between:
                between()
            with e.Fori(half, 2 * half - 1) as i:
                for p in range(2):
                    main(i * 2 + p, p, False)
            for p in range(2):
                main(CHUNKS - 2 + p, p, p == 1)

        @block.sync
        def _(sp):
            def load_x(c):
                sp.dma_start(x_t[:, :, :], a["x_t"].rearrange("(k p) t -> p k t", p=P)[:, :, bass.ds(c * TC, TC)])\
                    .then_inc(s_x, 16)

            def load_rep(rep, row, c, g, done):
                sp.dma_start(rep[:, g * GS:(g + 1) * GS, :],
                             a["bc"][bass.ds(c, 1), row + g * GS:row + (g + 1) * GS, :]
                             .broadcast_to([P, GS, TC])).then_inc(done[g], 16)

            def store_bc(c):
                sp.wait_ge(s_bc, c + 1)
                sp.dma_start(a["bc"][bass.ds(c, 1), :, :].rearrange("a s t -> (a s) t"), bc[:, :]).then_inc(s_bcd, 16)

            def load_bc_rep(c, g):
                sp.wait_ge(s_dbu, c * GROUPS + 7 * NG + g + 1 + DBU_CREDIT)
                load_rep(b_rep, 0, c + 1, g, s_b)
                sp.wait_ge(s_hc, c * GROUPS + 7 * NG + g + 1)
                load_rep(c_rep, NSTATE, c + 1, g, s_c)

            def store_y(c, j):
                n = c * NJ + j
                sp.wait_ge(s_y, n + 1 + Y_CREDIT)
                sp.dma_start(a["y_t"][j * P:(j + 1) * P, bass.ds(c * TC, TC)], y[:, j % 2, :])\
                    .then_inc(s_yout[j % 2], 16)

            for q in range(2):
                sp.sem_inc(s_yout[q], STORE_CREDIT)
            load_x(0)
            sp.dma_start(pieces[0][0], pieces[0][1]).then_inc(s_w[0], 16)
            sp.dma_start(b_in[:, :], a["b_in"]).then_inc(s_small, 16)
            sp.dma_start(w_xp32[:, :, :], a["w_xproj"].rearrange("(k p) n -> p k n", p=P)).then_inc(s_small, 16)
            sp.dma_start(b_xp[:, :], a["b_xproj"]).then_inc(s_small, 16)
            sp.dma_start(decay[:, :, :], a["a_log"].rearrange("(j p) s -> p j s", p=P)).then_inc(s_small, 16)
            sp.dma_start(b_dt[:, :], a["b_dt"]).then_inc(s_small, 16)
            sp.dma_start(d_skip[:, :], a["d_param"]).then_inc(s_small, 16)
            sp.dma_start(pieces[1][0], pieces[1][1]).then_inc(s_w[1], 16)
            for n in range(2, 4):
                sp.wait_ge(s_wl, (1, 3)[n - 2])
                sp.dma_start(pieces[n][0], pieces[n][1]).then_inc(s_w[n], 16)
            sp.wait_ge(s_xl, 1)
            load_x(1)
            store_bc(0)
            sp.wait_ge(s_bcd, 16)
            for g in range(NG):
                load_rep(b_rep, 0, 0, g, s_b)
            for g in range(NG):
                load_rep(c_rep, NSTATE, 0, g, s_c)

            def main(c, p, last):
                for j in range(NJ):
                    if not last:
                        if j == 5:
                            store_bc(c + 1)
                        if j == 1 and not (isinstance(c, int) and c + 2 >= CHUNKS):
                            sp.wait_ge(s_xl, c + 2)
                            load_x(c + 2)
                        if j == 7:
                            sp.wait_ge(s_bcd, (c + 2) * 16)
                            for g in range(NG - 1):
                                load_bc_rep(c, g)
                    if j > 0:
                        store_y(c, j - 1)
                    elif not (isinstance(c, int) and c == 0):
                        store_y(c - 1, NJ - 1)
                if not last:
                    load_bc_rep(c, NG - 1)
                else:
                    store_y(c, NJ - 1)

            all_chunks(sp, main)
            for q in range(2):
                sp.wait_ge(s_yout[q], 16 * CHUNKS * NJ // 2 + STORE_CREDIT)

        @block.tensor
        def _(pe):
            def project(w, col, rhs, kn, dst, done, width=P):
                for k in range(kn):
                    last = split_product(nc, dst, [part[:, k, col:col + width] for part in w],
                                         [part[:, k, :] for part in rhs], k == 0, k == kn - 1)
                last.then_inc(done, 1)

            def side(c, p, j, g):
                first = isinstance(c, int) and c == 0
                x = [part[:, p, :, :] for part in x16]
                if j == 0:
                    if g == 0:
                        pe.wait_ge(s_xl, c + 1)
                        if not first:
                            pe.wait_ge(s_abs, c * NJ)
                            pe.wait_ge(s_relu, c * NJ)
                    project(w_in, g * P, x, KD, proj[:, g, :], s_up)
                if j == 1:
                    if g == 0 and not first:
                        pe.wait_ge(s_z, c * NJ)
                    project(w_in, (4 + g) * P, x, KD, proj[:, 4 + g, :], s_up)
                if j == 2:
                    if g == 0:
                        pe.wait_ge(s_u, c * NJ + 4)
                    project(w_in, INNER + g * P, x, KD, proj[:, g, :], s_zp)
                if j == 3:
                    if g == 0:
                        pe.wait_ge(s_ul, c * 2 + 2)
                        if not first:
                            pe.wait_ge(s_bc, c)
                        project(w_xp, 0, u16, NJ, bc_ps[:, 0:TC], s_bcp, 2 * NSTATE)
                    if g in (1, 3):
                        project(w_dt, g // 2 * P, u16, NJ, proj[:, 4 + g // 2, :], s_dtp)
                if j in (4, 5, 6) and g in (0, 2):
                    t = 2 * (j - 3) + g // 2
                    if j == 5 and g == 0:
                        pe.wait_ge(s_z, c * NJ + 4)
                    project(w_dt, t * P, u16, NJ, proj[:, (t + 4) % NJ, :], s_dtp)
                if j == 7:
                    if g == 0:
                        pe.wait_ge(s_abs, c * NJ + 4)
                        pe.wait_ge(s_relu, c * NJ + 4)
                    project(w_in, INNER + (4 + g) * P, x, KD, proj[:, 4 + g, :], s_zp)

            def sums(c, j, g):
                n = c * NJ + j
                if g == 0:
                    pe.wait_ge(s_gate, n + 1)
                pe.wait_ge(s_hc, n * NG + g + 1)
                for s in range(GS):
                    last = nc.tensor.matmul(y_ps[:, j % 2, 0:TC], a["ident"][:, :], h[:, (j * NG + g) % RING, s, :],
                                            start=(g == 0 and s == 0), stop=(g == NG - 1 and s == GS - 1))
                last.then_inc(s_sum, 1)

            pe.sem_inc(s_sum, SUM_CREDIT)
            for j in range(NJ):
                pe.wait_ge(s_wl, (1, 1, 3, 5, 5, 5, 5, 5)[j])
                for g in range(NG):
                    side(0, 0, j, g)
            pe.wait_ge(a["s_ident"], 2)

            def main(c, p, last):
                for j in range(NJ):
                    for g in range(NG):
                        if not last:
                            side(c + 1, 1 - p, j, g)
                        sums(c, j, g)

            all_chunks(pe, main)

        @block.scalar
        def _(act):
            def silu(c, t, dst, col, psum_sem, done):
                act.wait_ge(psum_sem, c * NJ + t // 2 * 2 + 2)
                nc.scalar.activation(dst, proj[:, t, :], ACT.Silu, bias=b_in[:, col:col + 1], scale=UNSCALE)\
                    .then_inc(done, 1)

            def silu_u(c, p, t):
                silu(c, t, u[:, p, t, :], t, s_up, s_u)

            def u_high(c, p, half):
                tiles = slice(4 * half, 4 * half + 4)
                act.wait_ge(s_u, c * NJ + 4 * half + 4)
                nc.scalar.activation(u16[0][:, tiles, :], u[:, p, tiles, :], ACT.Copy).then_inc(s_uh, 1)

            def x_high(c, p):
                act.wait_ge(s_x, (c + 1) * 16)
                nc.scalar.activation(x16[0][:, p, :, :], x_t[:, :, :], ACT.Copy).then_inc(s_xh, 1)

            def silu_z(c, t):
                silu(c, t, z[:, t, :], NJ + t, s_zp, s_z)

            def evacuate_bc(c):
                act.wait_ge(s_bcp, c + 1)
                if not (isinstance(c, int) and c == 0):
                    act.wait_ge(s_bcd, c * 16)
                nc.scalar.activation(bc[:, :], bc_ps[:, 0:TC], ACT.Identity, bias=b_xp[:, 0:1], scale=UNSCALE)\
                    .then_inc(s_bc, 1)

            def soft_exp(c, t0):
                s0 = t0 % 4
                for t in range(t0, t0 + 2):
                    slot = t + 4 if t < 4 else t - 4
                    act.wait_ge(s_dtp, c * NJ + t // 2 * 2 + 2)
                    nc.scalar.activation(soft[:, t % 4, :], proj[:, slot, :], ACT.Abs, bias=b_dt[:, t:t + 1],
                                         scale=UNSCALE).then_inc(s_abs, 1)
                act.wait_ge(s_abs, c * NJ + t0 + 2)
                nc.scalar.activation(soft[:, s0:s0 + 2, :], soft[:, s0:s0 + 2, :], ACT.Exp, scale=-1.0).then_inc(s_sexp, 1)

            def soft_ln(c, half):
                act.wait_ge(s_sexp, c * 4 + 2 * half + 2)
                nc.scalar.activation(soft[:, :, :], soft[:, :, :], ACT.Ln, bias=1.0).then_inc(s_soft, 1)

            def weights_high(n):
                act.wait_ge(s_w[n], 16)
                nc.scalar.activation(pieces[n][2], pieces[n][0], ACT.Copy, scale=W_SCALE).then_inc(s_wh, 1)

            x_high(0, 0)
            weights_high(0)
            act.wait_ge(s_small, 96)
            nc.scalar.activation(w_xp[0][:, :, :], w_xp32[:, :, :], ACT.Copy, scale=W_SCALE).then_inc(s_wh, 1)
            nc.scalar.activation(decay[:, :, :], decay[:, :, :], ACT.Exp).then_inc(s_const, 1)
            weights_high(1)
            for half in range(2):
                for t in range(4 * half, 4 * half + 4):
                    silu_u(0, 0, t)
                u_high(0, 0, half)
                weights_high(2 + half)
            for t in range(4):
                silu_z(0, t)
            evacuate_bc(0)
            soft_exp(0, 0)
            soft_exp(0, 2)
            soft_ln(0, 0)
            act.wait_ge(s_dt, 1)
            soft_exp(0, 4)
            act.wait_ge(s_const, 2)
            x_high(1, 1)

            def side(c, p, g, last):
                if g == 0:
                    soft_exp(c, 6)
                    soft_ln(c, 1)
                if g == 7:
                    act.wait_ge(s_y, c * NJ + Y_CREDIT)
                    for t in range(4, 8):
                        silu_z(c, t)
                if last:
                    return
                if g == 9:
                    act.wait_ge(s_gate, c * NJ + GATE_CREDIT)
                    for t in range(4):
                        silu_u(c + 1, 1 - p, t)
                    u_high(c + 1, 1 - p, 0)
                if g == 13:
                    for t in range(4, 8):
                        silu_u(c + 1, 1 - p, t)
                    u_high(c + 1, 1 - p, 1)
                if g == 16 and not (isinstance(c, int) and c + 2 >= CHUNKS):
                    act.wait_ge(s_zp, (c + 1) * NJ)
                    x_high(c + 2, p)
                if g == 18:
                    evacuate_bc(c + 1)
                if g == 21:
                    act.wait_ge(s_dt, c * 2 + 2)
                    soft_exp(c + 1, 0)
                if g == 23:
                    act.wait_ge(s_y, c * NJ + 4 + Y_CREDIT)
                    for t in range(4):
                        silu_z(c + 1, t)
                if g == 24:
                    soft_exp(c + 1, 2)
                    soft_ln(c + 1, 0)
                if g == 28:
                    act.wait_ge(s_dt, (c + 1) * 2 + 1)
                    soft_exp(c + 1, 4)

            def main(c, p, last):
                for g in range(GROUPS):
                    j = g // NG
                    if g in (0, GROUPS // 2):
                        act.wait_ge(s_dt, c * 2 + 1 + 2 * g // GROUPS)
                    act.wait_ge(s_scan, c * GROUPS + g + 1)
                    for s in range(GS):
                        st = g % NG * GS + s
                        last_exp = nc.scalar.activation(da[:, g % RING, s, :], dt[:, j, :], ACT.Exp,
                                                        scale=decay[:, j, st:st + 1])
                    last_exp.then_inc(s_da, 1)
                    side(c, p, g, last)

            all_chunks(act, main)

        @block.vector
        def _(dve):
            def relu(c, t0, t1, after_scan):
                for t in range(t0, t1):
                    slot = t + 4 if t < 4 else t - 4
                    dve.wait_ge(s_abs, c * NJ + t // 2 * 2 + 2)
                    if after_scan:
                        dve.wait_ge(s_da, (c - 1) * GROUPS + (t + 1) * NG)
                        dve.wait_ge(s_dtu, (c - 1) * NJ + t + 1)
                    nc.vector.tensor_scalar(dt[:, t, :], proj[:, slot, :], b_dt64[:, t:t + 1], 0.0, ALU.add, ALU.max)\
                        .then_inc(s_relu, 1)

            def add_soft(c, half):
                tiles = slice(4 * half, 4 * half + 4)
                dve.wait_ge(s_soft, c * 2 + half + 1)
                dve.wait_ge(s_relu, c * NJ + 4 * half + 4)
                nc.vector.scalar_tensor_tensor(dt[:, tiles, :], dt[:, tiles, :], UNSCALE, soft[:, :, :],
                                               ALU.mult, ALU.add).then_inc(s_dt, 1)

            def weights_low(high, stage, low, n):
                dve.wait_ge(s_wh, n + 1)
                nc.vector.scalar_tensor_tensor(low, stage, W_SCALE, high, ALU.mult, ALU.subtract).then_inc(s_wl, 1)

            def dbu(c, p, j, g):
                m = c * GROUPS + j * NG + g
                if g == 0:
                    dve.wait_ge(s_dtu, c * NJ + j + 1)
                if j == 0:
                    dve.wait_ge(s_b[g], (c + 1) * 16)
                dve.wait_ge(s_sum, m + 1)
                nc.vector.tensor_tensor(h[:, (j * NG + g) % RING, :, :],
                                        dtu[:, j % 2:j % 2 + 1, :].broadcast_to([P, GS, TC]),
                                        b_rep[:, g * GS:(g + 1) * GS, :], ALU.mult).then_inc(s_dbu, 1)

            def scans(c, j, g):
                m = c * GROUPS + j * NG + g
                r = (j * NG + g) % RING
                dve.wait_ge(s_da, m + 1)
                dve.wait_ge(s_dbu, m + 1 + DBU_CREDIT)
                dve.wait_ge(s_hl, m + 1)
                for s in range(GS):
                    st = g * GS + s
                    last = nc.vector.tensor_tensor_scan(h[:, r, s, :], da[:, r, s, :], h[:, r, s, :],
                                                        h_last[:, j, st:st + 1], ALU.mult, ALU.add)
                last.then_inc(s_scan, 1)

            def gate(c, p, j):
                n = c * NJ + j
                dve.wait_ge(s_sum, (n + 1) * NG + SUM_CREDIT)
                dve.wait_ge(s_yout[j % 2], (c * (NJ // 2) + j // 2) * 16 + STORE_CREDIT)
                nc.vector.scalar_tensor_tensor(y[:, j % 2, :], u[:, p, j, :], d_skip[:, j:j + 1], y_ps[:, j % 2, 0:TC],
                                               ALU.mult, ALU.add).then_inc(s_gate, 1)

            dve.sem_inc(s_dbu, DBU_CREDIT)
            dve.sem_inc(s_scan, SCAN_CREDIT)
            dve.sem_inc(s_gate, GATE_CREDIT)
            weights_low(pieces[0][2], pieces[0][0], pieces[0][3], 0)
            weights_low(w_xp[0][:, :, :], w_xp32[:, :, :], w_xp[1][:, :, :], 1)
            dve.wait_ge(s_const, 1)
            nc.vector.tensor_scalar(decay[:, :, :], decay[:, :, :], -1.0, None, ALU.mult).then_inc(s_const, 1)
            nc.vector.tensor_scalar(b_dt64[:, :], b_dt[:, :], W_SCALE, None, ALU.mult).then_inc(s_const, 1)
            for n in range(1, 4):
                weights_low(pieces[n][2], pieces[n][0], pieces[n][3], n + 1)
            dve.wait_ge(s_const, 3)
            relu(0, 0, 4, False)
            add_soft(0, 0)
            relu(0, 4, 8, False)
            dbu(0, 0, 0, 0)
            dve.wait_ge(s_hz, 2)

            def main(c, p, last):
                for j in range(NJ):
                    for g in range(NG):
                        if g < NG - 1:
                            dbu(c, p, j, g + 1)
                        elif j < NJ - 1:
                            dbu(c, p, j + 1, 0)
                        elif not last:
                            dbu(c + 1, 1 - p, 0, 0)
                        scans(c, j, g)
                        if g == 2:
                            if j > 0:
                                gate(c, p, j - 1)
                            elif not (isinstance(c, int) and c == 0):
                                gate(c - 1, 1 - p, NJ - 1)
                        if g == 2 and j == 0:
                            add_soft(c, 1)
                        if last:
                            continue
                        if j * NG + g in (20, 23, 27, 31):
                            t = 2 * (20, 23, 27, 31).index(j * NG + g)
                            relu(c + 1, t, t + 2, True)
                        if j * NG + g == 24:
                            add_soft(c + 1, 0)
                if last:
                    gate(c, p, NJ - 1)

            all_chunks(dve, main, lambda: dve.wait_ge(s_hz, 3))

        @block.gpsimd
        def _(pool):
            def dt_times_u(c, p, j):
                n = c * NJ + j
                if j in (0, 4):
                    pool.wait_ge(s_dt, c * 2 + 1 + j // 4)
                pool.wait_ge(s_u, n + 1)
                pool.wait_ge(s_dbu, n * NG + NG)
                nc.gpsimd.tensor_tensor(dtu[:, j % 2, :], dt[:, j, :], u[:, p, j, :], ALU.mult).then_inc(s_dtu, 1)

            def finish_y(c, p, j):
                n = c * NJ + j
                pool.wait_ge(s_gate, n + 1 + GATE_CREDIT)
                pool.wait_ge(s_z, n + 1)
                nc.gpsimd.tensor_tensor(y[:, j % 2, :], y[:, j % 2, :], z[:, j, :], ALU.mult).then_inc(s_y, 1)

            def x_low(c, p):
                pool.wait_ge(s_xh, c + 1)
                nc.gpsimd.tensor_tensor(x16[1][:, p, :, :], x_t[:, :, :], x16[0][:, p, :, :], ALU.subtract).then_inc(s_xl, 1)

            def u_low(c, p, half):
                tiles = slice(4 * half, 4 * half + 4)
                pool.wait_ge(s_uh, c * 2 + half + 1)
                nc.gpsimd.tensor_tensor(u16[1][:, tiles, :], u[:, p, tiles, :], u16[0][:, tiles, :], ALU.subtract)\
                    .then_inc(s_ul, 1)

            def clear_h_last():
                nc.gpsimd.memset(h_last[:, :, :], 0.0).then_inc(s_hz, 1)

            pool.sem_inc(s_y, Y_CREDIT)
            pool.sem_inc(s_hl, GROUPS)
            nc.gpsimd.memset(a["ident"][:, :], 0.0).then_inc(a["s_ident"], 1)
            pool.wait_ge(a["s_ident"], 1)
            nc.gpsimd.affine_select(out=a["ident"][:, :], in_=a["ident"][:, :], compare_op=ALU.not_equal, fill=1.0,
                                    base=0, pattern=[[-1, P]], channel_multiplier=1).then_inc(a["s_ident"], 1)
            nc.gpsimd.memset(zeros[:, :], 0.0).then_inc(s_hz, 1)
            clear_h_last()
            x_low(0, 0)
            u_low(0, 0, 0)
            u_low(0, 0, 1)
            pool.wait_ge(s_hz, 2)
            x_low(1, 1)
            dt_times_u(0, 0, 0)

            def main(c, p, last):
                for j in range(NJ):
                    for g in range(NG):
                        m = c * GROUPS + j * NG + g
                        r = (j * NG + g) % RING
                        pool.wait_ge(s_scan, m + 1 + SCAN_CREDIT)
                        nc.gpsimd.tensor_tensor(h_last[:, j, g * GS:(g + 1) * GS], h[:, r, :, TC - 1], zeros[:, :],
                                                ALU.add).then_inc(s_hl, 1)
                        if j == 0:
                            pool.wait_ge(s_c[g], (c + 1) * 16)
                        pool.wait_ge(s_hl, m + 1 + GROUPS)
                        nc.gpsimd.tensor_tensor(h[:, r, :, :], h[:, r, :, :], c_rep[:, g * GS:(g + 1) * GS, :], ALU.mult)\
                            .then_inc(s_hc, 1)
                        if g == 0:
                            if j < NJ - 1:
                                dt_times_u(c, p, j + 1)
                            elif not last:
                                dt_times_u(c + 1, 1 - p, 0)
                        if not last and j * NG + g in (8, 11):
                            u_low(c + 1, 1 - p, (8, 11).index(j * NG + g))
                        if not last and j * NG + g == 20 and not (isinstance(c, int) and c + 2 >= CHUNKS):
                            x_low(c + 2, p)
                        if g == 3:
                            if j > 0:
                                finish_y(c, p, j - 1)
                            elif not (isinstance(c, int) and c == 0):
                                finish_y(c - 1, 1 - p, NJ - 1)
                if last:
                    finish_y(c, p, NJ - 1)

            def between():
                pool.wait_ge(s_hl, (PER_BATCH + 1) * GROUPS)
                clear_h_last()

            all_chunks(pool, main, between)


LANES = P // DK
HU = HEADS // LANES
NT = TC // P
NU = NF // 2
TWO_PI = 2.0 * math.pi
ROUND = 1.5 * 2.0 ** 23
MASKED = 1.0e9


def attention_ffn_phase(nc, a):
    with ExitStack() as ctx:
        def sb(name, shape, dt=FP32):
            return ctx.enter_context(nc.sbuf_tensor(name, shape, dt))

        def ps(name, shape):
            return ctx.enter_context(nc.psum_tensor(name, shape, FP32))

        def sem(name):
            return ctx.enter_context(nc.semaphore(name))

        ident = a["ident"]
        w_out = sb("w_out", [P, NJ, D])
        w_q = sb("w_q", [P, KD, D])
        w_o = sb("w_o", [P, KD, D])
        w_1 = sb("w_1", [P, KD, FF])
        w_2 = sb("w_2", [P, NF, D])
        rows = sb("rows", [P, 3, D])
        b_q = sb("b_q", [P, KD])
        b_k = sb("b_k", [P, KD])
        b_1 = sb("b_1", [P, NF])
        k_t = sb("k_t", [P, BATCH, KD, CTX])
        v = sb("v", [CTX, BATCH, D])
        theta = sb("theta", [P, NF])
        w_re = sb("w_re", [P, NF])
        w_im = sb("w_im", [P, NF])
        turns = sb("turns", [P, NF])
        gain = sb("gain", [P, NF])
        tmp = sb("tmp", [P, 3, NF])
        eps = sb("eps", [P, 1])
        y_t = sb("y_t", [P, NJ, TC])
        x_in = sb("x_in", [P, NT, D])
        x1 = sb("x1", [P, NT, D])
        x2 = sb("x2", [P, NT, D])
        x3 = sb("x3", [P, NT, D])
        xa_t = sb("xa_t", [P, KD, TC])
        q_t = sb("q_t", [P, KD, TC])
        x2_t = sb("x2_t", [P, KD, TC])
        stats = sb("stats", [P, 3, NT, 6])
        mv = sb("mv", [P, 3, NT, 2])
        std = sb("std", [P, 3, NT])
        rstd = sb("rstd", [P, 3, NT])
        mask_i = sb("mask_i", [P, NT, CTX], INT32)
        keep = sb("keep", [P, NT, CTX])
        fill = sb("fill", [P, NT, CTX])
        pr = sb("pr", [P, NT, HEADS, CTX])
        smax = sb("smax", [P, NT, HEADS])
        ssum = sb("ssum", [P, NT, HEADS])
        sinv = sb("sinv", [P, NT, HEADS])
        p_t = sb("p_t", [P, HEADS, TC])
        act_t = sb("act_t", [P, NF, TC])
        hid = sb("hid", [P, 3, 2, TC])
        arg = sb("arg", [P, 3, 2, TC])
        whole = sb("whole", [P, 2, 2, TC])

        nat = ps("nat", [P, 2, D])
        tr = ps("tr", [P, KD, TC])
        fps = ps("fps", [P, 2, 2, TC])
        sps = ps("sps", [P, 2, 512])
        ctx_t = act_t[:, 0:3, :].rearrange("p a b -> p (a b)")[:, 0:KD * BATCH * CTX]\
            .rearrange("p (k b t) -> p k b t", k=KD, b=BATCH)
        wk = p_t[:, 0:8, :].rearrange("p a b -> p (a b)").rearrange("p (k n) -> p k n", k=KD)
        wv = p_t[:, 8:16, :].rearrange("p a b -> p (a b)").rearrange("p (k n) -> p k n", k=KD)

        s_wkv, s_wout, s_wq, s_w1, s_w2 = (sem(f"b_{n}_loaded") for n in ("wkv", "wout", "wq_wo", "w1", "w2"))
        s_small, s_rows = sem("b_small_loaded"), sem("b_rows_loaded")
        s_yt, s_xin, s_mask = sem("b_yt_loaded"), sem("b_x_loaded"), sem("b_mask_loaded")
        s_out = sem("b_out_stored")
        s_kvp, s_kv = sem("b_kv_psum"), sem("b_kv_ready")
        s_chain, s_ss, s_tick = sem("b_param_chain"), sem("b_softmax_sums"), sem("b_statistics_awaited")
        s_par, s_parv = sem("b_param_act"), sem("b_param_dve")
        s_nat = {n: sem(f"b_{n}_psum") for n in ("outproj", "wo", "w2")}
        s_r = {n: sem(f"b_{n}_residual") for n in ("outproj", "wo", "w2")}
        s_st, s_mv, s_sd, s_rs, s_x = ({n: sem(f"b_{n}_{w}") for n in ("outproj", "wo", "w2")}
                                       for w in ("stats", "meanvar", "std", "rstd", "normed"))
        s_xb = {n: sem(f"b_{n}_bias_added") for n in ("xin", "outproj", "wo")}
        s_x1tp, s_x1t, s_qp, s_q = sem("b_x1t_psum"), sem("b_x1t"), sem("b_q_psum"), sem("b_q")
        s_x2tp, s_x2t = sem("b_x2t_psum"), sem("b_x2t")
        s_keep = sem("b_keep_ready")
        s_scp, s_sc = sem("b_scores_psum"), sem("b_scores_read")
        s_sma, s_smb = sem("b_scores_less_maximum"), sem("b_sums_inverse")
        s_pexp, s_pn = sem("b_exp_done"), sem("b_probs_ready")
        s_ptp, s_pt = sem("b_pt_psum"), sem("b_pt")
        s_avp, s_av = sem("b_av_psum"), sem("b_av")
        s_hp, s_h, s_arg, s_wh, s_fr, s_sin, s_mix, s_act = (sem(f"b_ffn_{n}") for n in (
            "psum", "hidden", "argument", "whole", "fraction", "sine", "mixed", "act"))

        block = ctx.enter_context(nc.Block())

        def all_chunks(e, front_back):
            front_back(0, 0, True, False)
            front_back(1, 0, True, True)
            with e.Fori(2, PER_BATCH) as c:
                front_back(c, 0, True, True)
            with e.Fori(PER_BATCH, CHUNKS - 1) as c:
                front_back(c, 1, True, True)
            front_back(CHUNKS - 1, 1, True, True)
            front_back(CHUNKS, 1, False, True)

        @block.sync
        def _(sp):
            def load(dst, src, s):
                sp.dma_start(dst, src).then_inc(s, 16)

            load(ctx_t[:, :, :, :], a["ctx_t"].rearrange("(k p) b t -> p k b t", p=P), s_wkv)
            load(wk, a["wk_t"].rearrange("(k p) n -> p k n", p=P), s_wkv)
            load(wv, a["wv_t"].rearrange("(k p) n -> p k n", p=P), s_wkv)
            load(b_k[:, :], a["b_k"], s_wkv)
            load(rows[:, 0, :], a["b_v"].broadcast_to([P, D]), s_wkv)
            load(y_t[:, :, :], a["y_t"].rearrange("(j p) t -> p j t", p=P)[:, :, 0:TC], s_yt)
            load(w_out[:, :, :], a["w_out"].rearrange("(k p) n -> p k n", p=P), s_wout)
            load(x_in[:, :, :], a["x"].rearrange("(t p) d -> p t d", p=P)[:, 0:NT, :], s_xin)
            for dst, name in ((b_q, "b_q"), (b_1, "b_1"), (theta, "theta"), (w_re, "w_re"), (w_im, "w_im")):
                load(dst[:, :], a[name], s_small)
            load(w_q[:, :, :], a["wq_t"].rearrange("(k p) n -> p k n", p=P), s_wq)
            load(w_o[:, :, :], a["wo_t"].rearrange("(k p) n -> p k n", p=P), s_wq)
            sp.wait_ge(s_kv, 4 * BATCH + BATCH)
            for n, name in enumerate(("b_out", "b_o", "b_2")):
                load(rows[:, n, :], a[name].broadcast_to([P, D]), s_rows)
            load(w_1[:, :, :], a["w_1"].rearrange("(k p) n -> p k n", p=P), s_w1)
            load(w_2[:, :, :], a["w_2"].rearrange("(k p) n -> p k n", p=P), s_w2)

            def front_back(c, batch, front, back):
                if front:
                    sp.wait_ge(s_keep, c * 2)
                    load(mask_i[:, :, :], a["mask"].rearrange("(t p) s -> p t s", p=P)
                         [:, bass.ds((c - batch * PER_BATCH) * NT, NT), :], s_mask)
                if front and not (isinstance(c, int) and c == CHUNKS - 1):
                    sp.wait_ge(s_nat["outproj"], (c + 1) * NT)
                    load(y_t[:, :, :], a["y_t"].rearrange("(j p) t -> p j t", p=P)[:, :, bass.ds((c + 1) * TC, TC)], s_yt)
                    sp.wait_ge(s_r["outproj"], (c + 1) * NT)
                    load(x_in[:, :, :], a["x"].rearrange("(t p) d -> p t d", p=P)[:, bass.ds((c + 1) * NT, NT), :], s_xin)
                if back:
                    sp.wait_ge(s_x["w2"], c * NT)
                    load(a["out"].rearrange("(t p) d -> p t d", p=P)[:, bass.ds((c - 1) * NT, NT), :], x3[:, :, :], s_out)

            all_chunks(sp, front_back)
            sp.wait_ge(s_out, CHUNKS * 16)

        @block.tensor
        def _(pe):
            mm = nc.tensor.matmul
            pe.wait_ge(s_wkv, 80)
            for b in range(BATCH):
                for t in range(KD):
                    for k in range(KD):
                        last = mm(sps[:, b, t * CTX:(t + 1) * CTX], wk[:, k, t * P:(t + 1) * P], ctx_t[:, k, b, :],
                                  start=(k == 0), stop=(k == KD - 1))
                    last.then_inc(s_kvp, 1)
                for k in range(KD):
                    last = mm(nat[0:CTX, b, :], ctx_t[:, k, b, :], wv[:, k, :], start=(k == 0), stop=(k == KD - 1))
                last.then_inc(s_kvp, 1)

            def transposes(src, dst, done):
                for t in range(NT):
                    for k in range(KD):
                        last = nc.tensor.transpose(dst[:, k, t * P:(t + 1) * P], src[:, t, k * P:(k + 1) * P], ident[:, :])
                last.then_inc(done, 1)

            def natural(lhs, w, kn, t, k0, k1, done):
                for k in range(k0, k1):
                    last = mm(nat[:, t, :], lhs[:, k, t * P:(t + 1) * P], w[:, k, :], start=(k == 0), stop=(k == kn - 1))
                if k1 == kn:
                    last.then_inc(done, 1)

            def hidden(b, n):
                if n == 0:
                    pe.wait_ge(s_x2t, b + 1)
                if n >= 2:
                    pe.wait_ge(s_h, b * NF + 2 * (n - 1))
                else:
                    pe.wait_ge(s_h, b * NF)
                for i in range(2):
                    f = 2 * n + i
                    for k in range(KD):
                        last = mm(fps[:, n % 2, i, :], w_1[:, k, f * P:(f + 1) * P], x2_t[:, k, :],
                                  start=(k == 0), stop=(k == KD - 1))
                    last.then_inc(s_hp, 1)

            def scores(c, t, batch):
                for lane in range(LANES):
                    unit = t * LANES + lane
                    if unit < 2:
                        pe.wait_ge(s_pt, c * 8)
                    else:
                        pe.wait_ge(s_sc, c * 8 + unit - 1)
                    rows_of = slice(lane * DK, (lane + 1) * DK)
                    for i in range(HU):
                        last = mm(sps[:, unit % 2, i * CTX:(i + 1) * CTX],
                                  q_t[rows_of, i, t * P:(t + 1) * P], k_t[rows_of, batch, i, :],
                                  start=True, stop=True)
                    last.then_inc(s_scp, 1)

            def probs_t(c, t):
                pe.wait_ge(s_pn, c * NT + t + 1)
                for n in range(4):
                    unit = t * 4 + n
                    if unit < 2:
                        pe.wait_ge(s_sc, c * 8 + 8)
                    else:
                        pe.wait_ge(s_pt, c * 8 + unit - 1)
                    for i in range(4):
                        last = nc.tensor.transpose(sps[0:CTX, unit % 2, i * P:(i + 1) * P], pr[:, t, 4 * n + i, :], ident[:, :])
                    last.then_inc(s_ptp, 1)

            def front_back(c, batch, front, back):
                b = c - 1
                if front:
                    pe.wait_ge(s_wout, 16)
                    pe.wait_ge(s_yt, (c + 1) * 16)
                    pe.wait_ge(s_r["wo"], c * NT)
                    natural(y_t, w_out, NJ, 0, 0, NJ, s_nat["outproj"])
                if back:
                    pe.wait_ge(s_x["wo"], c * NT)
                    pe.wait_ge(s_av, c)
                    transposes(x2, tr, s_x2tp)
                if front:
                    natural(y_t, w_out, NJ, 1, 0, NJ, s_nat["outproj"])
                if back:
                    pe.wait_ge(s_w1, 16)
                    for n in range(4):
                        hidden(b, n)
                if front:
                    pe.wait_ge(s_x["outproj"], (c + 1) * NT)
                    pe.wait_ge(s_x2t, c)
                    transposes(x1, tr, s_x1tp)
                if back:
                    hidden(b, 4)
                if front:
                    pe.wait_ge(s_wq, 32)
                    pe.wait_ge(s_x1t, c + 1)
                    for t in range(KD):
                        for k in range(KD):
                            last = mm(tr[:, t, :], w_q[:, k, t * P:(t + 1) * P], xa_t[:, k, :], start=(k == 0), stop=(k == KD - 1))
                        last.then_inc(s_qp, 1)
                if back:
                    hidden(b, 5)
                if front:
                    pe.wait_ge(s_q, (c + 1) * KD)
                    scores(c, 0, batch)
                if back:
                    hidden(b, 6)
                if front:
                    scores(c, 1, batch)
                if back:
                    hidden(b, 7)
                    pe.wait_ge(s_w2, 16)
                    if front:
                        pe.wait_ge(s_r["outproj"], (c + 1) * NT)
                    else:
                        pe.wait_ge(s_r["wo"], c * NT)
                    for n in range(NU):
                        pe.wait_ge(s_act, b * NU + n + 1)
                        natural(act_t, w_2, NF, 0, 2 * n, 2 * n + 2, s_nat["w2"])
                if front:
                    probs_t(c, 0)
                if back:
                    natural(act_t, w_2, NF, 1, 0, NF // 2, s_nat["w2"])
                if front:
                    probs_t(c, 1)
                if back:
                    natural(act_t, w_2, NF, 1, NF // 2, NF, s_nat["w2"])
                if front:
                    pe.wait_ge(s_pt, (c + 1) * 8)
                    for hh in range(HEADS):
                        r = 32 * (hh % 4)
                        last = mm(tr[r:r + DK, hh // 4, :], v[:, batch, hh * DK:(hh + 1) * DK],
                                  p_t[0:CTX, HU * (hh % 4) + hh // 4, :],
                                  start=True, stop=True)
                    last.then_inc(s_avp, 1)
                    pe.wait_ge(s_av, c + 1)
                    if back:
                        pe.wait_ge(s_r["w2"], c * NT)
                    else:
                        pe.wait_ge(s_r["outproj"], (c + 1) * NT)
                    for t in range(NT):
                        natural(xa_t, w_o, KD, t, 0, KD, s_nat["wo"])

            pe.wait_ge(s_kv, 5 * BATCH)
            all_chunks(pe, front_back)

        @block.scalar
        def _(act):
            act.wait_ge(s_wkv, 80)
            for b in range(BATCH):
                for t in range(KD):
                    act.wait_ge(s_kvp, b * 5 + KD)
                    nc.scalar.activation(k_t[:, b, t, :], sps[:, b, t * CTX:(t + 1) * CTX], ACT.Identity,
                                         bias=b_k[:, t:t + 1]).then_inc(s_kv, 1)
            act.wait_ge(s_small, 5 * 16)
            act.wait_ge(s_parv, 1)
            nc.scalar.activation(tmp[:, 0:2, :], tmp[:, 0:2, :], ACT.Sin, scale=6.283185).then_inc(s_par, 1)
            act.wait_ge(s_parv, 2)

            def deviation(n, i, c):
                act.wait_ge(s_mv[n], c + 1)
                nc.scalar.activation(std[:, i, :], mv[:, i, :, 1], ACT.Sqrt, bias=eps[:, 0:1]).then_inc(s_sd[n], 1)

            def hid_out(b, n):
                act.wait_ge(s_act, b * NU + n - 2) if n >= 3 else act.wait_ge(s_act, b * NU)
                for i in range(2):
                    f = 2 * n + i
                    act.wait_ge(s_hp, b * NF + 2 * n + 2)
                    nc.scalar.activation(hid[:, n % 3, i, :], fps[:, n % 2, i, :], ACT.Identity, bias=b_1[:, f:f + 1])\
                        .then_inc(s_h, 1)

            def sine(b, n):
                act.wait_ge(s_fr, b * NU + n + 1)
                nc.scalar.activation(arg[:, n % 3, :, :], arg[:, n % 3, :, :], ACT.Sin, scale=6.283185).then_inc(s_sin, 1)

            def relu(b, n):
                act.wait_ge(s_mix, b * NF + 2 * n + 2)
                if n == 0:
                    act.wait_ge(s_nat["w2"], b * NT)
                nc.scalar.activation(act_t[:, 2 * n:2 * n + 2, :], hid[:, n % 3, :, :], ACT.Relu).then_inc(s_act, 1)

            def exps(c, t):
                act.wait_ge(s_sma, (c * NT + t) * 3 + 3)
                nc.scalar.activation(pr[:, t, :, :], pr[:, t, :, :], ACT.Exp).then_inc(s_pexp, 1)

            def probs_out(c, t):
                for n in range(4):
                    act.wait_ge(s_ptp, c * 8 + t * 4 + n + 1)
                    if t == 0 and n == 0:
                        act.wait_ge(s_avp, c)
                    nc.scalar.activation(p_t[0:CTX, 4 * n:4 * n + 4, t * P:(t + 1) * P],
                                         sps[0:CTX, n % 2, :].rearrange("p (h t) -> p h t", h=4), ACT.Copy).then_inc(s_pt, 1)

            def front_back(c, batch, front, back):
                b = c - 1
                if back:
                    act.wait_ge(s_x2tp, c)
                    act.wait_ge(s_hp, b * NF)
                    nc.scalar.activation(x2_t[:, :, :], tr[:, :, :], ACT.Copy).then_inc(s_x2t, 1)
                if front:
                    deviation("outproj", 0, c)
                if back:
                    for n in range(4):
                        hid_out(b, n)
                        if n >= 1:
                            sine(b, n - 1)
                        if n >= 2:
                            relu(b, n - 2)
                if front:
                    act.wait_ge(s_x1tp, c + 1)
                    act.wait_ge(s_nat["wo"], c * NT)
                    nc.scalar.activation(xa_t[:, :, :], tr[:, :, :], ACT.Copy).then_inc(s_x1t, 1)
                if back:
                    hid_out(b, 4)
                    sine(b, 3)
                    relu(b, 2)
                if front:
                    for t in range(KD):
                        act.wait_ge(s_qp, c * KD + t // 2 * 2 + 2)
                        if t == 0:
                            act.wait_ge(s_scp, c * 8)
                        nc.scalar.activation(q_t[:, t, :], tr[:, t, :], ACT.Identity, bias=b_q[:, t:t + 1],
                                             scale=DK ** -0.5).then_inc(s_q, 1)
                if back:
                    hid_out(b, 5)
                    sine(b, 4)
                    relu(b, 3)
                    hid_out(b, 6)
                    sine(b, 5)
                    relu(b, 4)
                if front:
                    exps(c, 0)
                if back:
                    relu(b, 5)
                    hid_out(b, 7)
                if front:
                    exps(c, 1)
                if back:
                    sine(b, 6)
                    sine(b, 7)
                    relu(b, 6)
                    relu(b, 7)
                if front:
                    probs_out(c, 0)
                    probs_out(c, 1)
                    act.wait_ge(s_avp, c + 1)
                    act.wait_ge(s_qp, (c + 1) * KD)
                    nc.scalar.activation(xa_t[:, :, :], tr[:, :, :], ACT.Copy).then_inc(s_av, 1)
                if back:
                    deviation("w2", 2, b)
                if front:
                    deviation("wo", 1, c)

            all_chunks(act, front_back)

        @block.vector
        def _(dve):
            chain = {"n": 0}

            def link(ins):
                chain["n"] += 1
                ins.then_inc(s_chain, 1)
                dve.wait_ge(s_chain, chain["n"])

            for b in range(BATCH):
                dve.wait_ge(s_wkv, 80)
                dve.wait_ge(s_kvp, b * 5 + 5)
                nc.vector.tensor_tensor(v[:, b, :], nat[0:CTX, b, :], rows[0:CTX, 0, :], ALU.add).then_inc(s_kv, 1)
            dve.wait_ge(s_small, 5 * 16)
            link(nc.vector.memset(eps[:, :], EPS))
            link(nc.vector.tensor_scalar(tmp[:, 2, :], theta[:, :], 1.0 / TWO_PI, ROUND, ALU.mult, ALU.add))
            link(nc.vector.tensor_scalar(tmp[:, 2, :], tmp[:, 2, :], ROUND, None, ALU.subtract))
            link(nc.vector.scalar_tensor_tensor(theta[:, :], tmp[:, 2, :], -6.28125, theta[:, :], ALU.mult, ALU.add))
            link(nc.vector.scalar_tensor_tensor(theta[:, :], tmp[:, 2, :], -(TWO_PI - 6.28125), theta[:, :], ALU.mult, ALU.add))
            link(nc.vector.tensor_scalar(turns[:, :], theta[:, :], 1.0 / TWO_PI, None, ALU.mult))
            link(nc.vector.tensor_scalar(tmp[:, 0, :], turns[:, :], 0.25, None, ALU.add))
            link(nc.vector.tensor_copy(tmp[:, 1, :], turns[:, :]))
            for i in range(2):
                link(nc.vector.tensor_scalar(tmp[:, 2, :], tmp[:, i, :], ROUND, ROUND, ALU.add, ALU.subtract))
                last = nc.vector.tensor_tensor(tmp[:, i, :], tmp[:, i, :], tmp[:, 2, :], ALU.subtract)
                if i == 0:
                    link(last)
            last.then_inc(s_parv, 1)
            link(nc.vector.tensor_scalar(b_q[:, :], b_q[:, :], DK ** -0.5, None, ALU.mult))
            dve.wait_ge(s_par, 1)
            link(nc.vector.tensor_tensor(tmp[:, 0, :], tmp[:, 0, :], w_re[:, :], ALU.mult))
            link(nc.vector.tensor_tensor(tmp[:, 1, :], tmp[:, 1, :], w_im[:, :], ALU.mult))
            link(nc.vector.tensor_tensor(tmp[:, 0, :], tmp[:, 0, :], tmp[:, 1, :], ALU.add))
            link(nc.vector.tensor_scalar(tmp[:, 0, :], tmp[:, 0, :], 0.1, None, ALU.mult))
            nc.vector.tensor_tensor(gain[:, :], tmp[:, 0, :], w_im[:, :], ALU.mult).then_inc(s_parv, 1)
            dve.wait_ge(s_parv, 2)

            def residual(n, c, x, xb_sem, into):
                for t in range(NT):
                    dve.wait_ge(s_nat[n], c * NT + t + 1)
                    if t == 0:
                        dve.wait_ge(xb_sem, c + 1)
                    nc.vector.tensor_tensor(into[:, t, :], nat[:, t, :], x[:, t, :], ALU.add).then_inc(s_r[n], 1)

            def statistics(n, i, c, x):
                for t in range(NT):
                    dve.wait_ge(s_r[n], c * NT + t + 1)
                    nc.vector.bn_stats(stats[:, i, t, :], x[:, t, :]).then_inc(s_st[n], 1)
                dve.wait_ge(s_st[n], (c + 1) * NT)
                dve.sem_inc(s_tick, 1)
                for t in range(NT):
                    last = nc.vector.bn_aggr(mv[:, i, t, :], stats[:, i, t, :])
                last.then_inc(s_mv[n], 1)

            def normalize(n, i, c, x):
                dve.wait_ge(s_sd[n], c + 1)
                nc.vector.reciprocal(rstd[:, i, :], std[:, i, :]).then_inc(s_rs[n], 1)
                dve.wait_ge(s_rs[n], c + 1)
                for t in range(NT):
                    nc.vector.tensor_scalar(x[:, t, :], x[:, t, :], mv[:, i, t, 0:1], rstd[:, i, t:t + 1],
                                            ALU.subtract, ALU.mult).then_inc(s_x[n], 1)

            def arguments(b, n):
                for i in range(2):
                    f = 2 * n + i
                    dve.wait_ge(s_h, b * NF + f + 1)
                    nc.vector.tensor_scalar(arg[:, n % 3, i, :], hid[:, n % 3, i, :], 0.1 / TWO_PI, turns[:, f:f + 1],
                                            ALU.mult, ALU.add).then_inc(s_arg, 1)
                dve.wait_ge(s_arg, b * NF + 2 * n + 2)
                nc.vector.tensor_scalar(whole[:, n % 2, :, :], arg[:, n % 3, :, :], ROUND, ROUND, ALU.add, ALU.subtract)\
                    .then_inc(s_wh, 1)

            def mix(b, n):
                dve.wait_ge(s_sin, b * NU + n + 1)
                for i in range(2):
                    f = 2 * n + i
                    nc.vector.scalar_tensor_tensor(hid[:, n % 3, i, :], arg[:, n % 3, i, :], gain[:, f:f + 1],
                                                   hid[:, n % 3, i, :], ALU.mult, ALU.add).then_inc(s_mix, 1)

            def mask(c):
                dve.wait_ge(s_mask, (c + 1) * 16)
                nc.vector.tensor_scalar(keep[:, :, :], mask_i[:, :, :], 0.0, None, ALU.not_equal).then_inc(s_keep, 1)
                dve.wait_ge(s_keep, c * 2 + 1)
                nc.vector.tensor_scalar(fill[:, :, :], keep[:, :, :], 1.0, MASKED, ALU.subtract, ALU.mult).then_inc(s_keep, 1)

            def softmax_a(c, t):
                base = (c * NT + t) * 3
                for lane in range(LANES):
                    unit = t * LANES + lane
                    dve.wait_ge(s_scp, c * 8 + unit + 1)
                    if lane == 0:
                        dve.wait_ge(s_keep, c * 2 + 2)
                    nc.vector.tensor_tensor(pr[:, t, HU * lane:HU * (lane + 1), :],
                                            sps[:, unit % 2, 0:HU * CTX].rearrange("p (h k) -> p h k", k=CTX),
                                            keep[:, t:t + 1, :].broadcast_to([P, HU, CTX]), ALU.mult).then_inc(s_sc, 1)
                dve.wait_ge(s_sc, c * 8 + (t + 1) * LANES)
                nc.vector.tensor_tensor(pr[:, t, :, :], pr[:, t, :, :], fill[:, t:t + 1, :].broadcast_to([P, HEADS, CTX]),
                                        ALU.add).then_inc(s_sma, 1)
                dve.wait_ge(s_sma, base + 1)
                nc.vector.tensor_reduce(smax[:, t, :], pr[:, t, :, :], AXIS_X, ALU.max).then_inc(s_sma, 1)
                dve.wait_ge(s_sma, base + 2)
                nc.vector.tensor_tensor(pr[:, t, :, :], pr[:, t, :, :],
                                        smax[:, t, :].unsqueeze(2).broadcast_to([P, HEADS, CTX]), ALU.subtract)\
                    .then_inc(s_sma, 1)

            def softmax_b(c, t):
                dve.wait_ge(s_pexp, c * NT + t + 1)
                nc.vector.tensor_reduce(ssum[:, t, :], pr[:, t, :, :], AXIS_X, ALU.add).then_inc(s_ss, 1)
                dve.wait_ge(s_ss, c * NT + t + 1)
                nc.vector.reciprocal(sinv[:, t, :], ssum[:, t, :]).then_inc(s_smb, 1)


            def front_back(c, batch, front, back):
                b = c - 1
                if front:
                    mask(c)
                    residual("outproj", c, x_in, s_xb["xin"], x1)
                    statistics("outproj", 0, c, x1)
                    normalize("outproj", 0, c, x1)
                if back:
                    for n in range(6):
                        arguments(b, n)
                        if n:
                            mix(b, n - 1)
                if front:
                    softmax_a(c, 0)
                if back:
                    arguments(b, 6)
                    mix(b, 5)
                if front:
                    softmax_a(c, 1)
                if back:
                    arguments(b, 7)
                    mix(b, 6)
                if front:
                    softmax_b(c, 0)
                if back:
                    mix(b, 7)
                if front:
                    softmax_b(c, 1)
                if back:
                    dve.wait_ge(s_out, b * 16)
                    residual("w2", b, x2, s_xb["wo"], x3)
                    statistics("w2", 2, b, x3)
                    normalize("w2", 2, b, x3)
                if front:
                    residual("wo", c, x1, s_xb["outproj"], x2)
                    statistics("wo", 1, c, x2)
                    normalize("wo", 1, c, x2)

            all_chunks(dve, front_back)

        @block.gpsimd
        def _(pool):
            def add_bias(x, row, done):
                nc.gpsimd.tensor_tensor(x[:, :, :], x[:, :, :], rows[:, row:row + 1, :].broadcast_to([P, NT, D]), ALU.add)\
                    .then_inc(done, 1)

            def fraction(b, n):
                pool.wait_ge(s_wh, b * NU + n + 1)
                nc.gpsimd.tensor_tensor(arg[:, n % 3, :, :], arg[:, n % 3, :, :], whole[:, n % 2, :, :], ALU.subtract)\
                    .then_inc(s_fr, 1)

            def probs(c, t):
                pool.wait_ge(s_smb, c * NT + t + 1)
                nc.gpsimd.tensor_tensor(pr[:, t, :, :], pr[:, t, :, :],
                                        sinv[:, t, :].unsqueeze(2).broadcast_to([P, HEADS, CTX]), ALU.mult).then_inc(s_pn, 1)

            pool.wait_ge(s_rows, 3 * 16)

            def front_back(c, batch, front, back):
                b = c - 1
                if back:
                    pool.wait_ge(s_x2tp, c)
                    add_bias(x2, 2, s_xb["wo"])
                if front:
                    pool.wait_ge(s_xin, (c + 1) * 16)
                    add_bias(x_in, 0, s_xb["xin"])
                if back:
                    for n in range(5):
                        fraction(b, n)
                if front:
                    pool.wait_ge(s_x1tp, c + 1)
                    add_bias(x1, 1, s_xb["outproj"])
                if back:
                    for n in range(5, 8):
                        fraction(b, n)
                if front:
                    for t in range(NT):
                        probs(c, t)

            all_chunks(pool, front_back)


def program(nc, a):
    with ExitStack() as ctx:
        ident = ctx.enter_context(nc.sbuf_tensor("ident", [P, P], FP32))
        a = dict(a, ident=ident,
                 s_ident=ctx.enter_context(nc.semaphore("identity_ready")))
        selective_scan_phase(nc, a)
        attention_ffn_phase(nc, a)


def kernel(**inputs):
    import numpy as np
    import concourse.bacc as bacc
    from concourse.bass_utils import run_bass_kernel_spmd

    def arr(name):
        return np.asarray(inputs[name])

    def columns(v):
        return np.ascontiguousarray(v.reshape(-1, P).T)

    x = arr("x").reshape(TOKENS, D)
    arrays = {
        "x": x,
        "x_t": x.T,
        "mask": arr("mask_1x1xSxS2_ik0")[0, 0],
        "ctx_t": arr("ctx_1024").transpose(2, 0, 1),
        "w_in": arr("L0_attn_W_in"), "b_in": columns(arr("L0_attn_b_in")),
        "w_xproj": arr("L0_attn_W_xproj"), "b_xproj": arr("L0_attn_b_xproj").reshape(-1, 1),
        "w_dt": arr("L0_attn_W_dt"), "b_dt": columns(arr("L0_attn_b_dt")),
        "a_log": arr("L0_attn_A_log"), "d_param": columns(arr("L0_attn_D_param")),
        "w_out": arr("L0_attn_W_out"), "b_out": arr("L0_attn_b_out").reshape(1, -1),
        "wq_t": arr("L0_xattn_wq_w").T, "wk_t": arr("L0_xattn_wk_w").T,
        "wv_t": arr("L0_xattn_wv_w").T, "wo_t": arr("L0_xattn_wo_w").T,
        "b_q": columns(arr("L0_xattn_wq_b")), "b_k": columns(arr("L0_xattn_wk_b")),
        "b_v": arr("L0_xattn_wv_b").reshape(1, -1), "b_o": arr("L0_xattn_wo_b").reshape(1, -1),
        "w_1": arr("L0_ffn_W1"), "b_1": columns(arr("L0_ffn_b1")),
        "theta": columns(arr("L0_ffn_quantum_phases")),
        "w_re": columns(arr("L0_ffn_quantum_weights_real")), "w_im": columns(arr("L0_ffn_quantum_weights_imag")),
        "w_2": arr("L0_ffn_W2"), "b_2": arr("L0_ffn_b2").reshape(1, -1),
    }
    nc = bacc.Bacc("TRN2", target_bir_lowering=False, num_devices=1)
    aps, sent = {}, {}
    for name, value in arrays.items():
        sent[f"dram_{name}"] = np.ascontiguousarray(value)
        aps[name] = nc.dram_tensor(f"dram_{name}", value.shape, mybir.dt.from_np(value.dtype), kind="ExternalInput").ap()
    aps["bc"] = nc.dram_tensor("bc_dram", (CHUNKS, 2 * NSTATE, TC), FP32, kind="Internal").ap()
    aps["y_t"] = nc.dram_tensor("y_t_dram", (INNER, TOKENS), FP32, kind="Internal").ap()
    aps["out"] = nc.dram_tensor("result", (TOKENS, D), FP32, kind="ExternalOutput").ap()
    program(nc, aps)
    r = run_bass_kernel_spmd(nc, [sent], core_ids=[0])
    return r.results[0]["result"].reshape(BATCH, SEQ, D)
```

```python
import math
from contextlib import ExitStack

import concourse.bass as bass
from concourse import mybir

FP32 = mybir.dt.float32
FP16 = mybir.dt.float16
INT32 = mybir.dt.int32
ALU = mybir.AluOpType
ACT = mybir.ActivationFunctionType
AXIS_X = mybir.AxisListType.X

P = 128
BATCH, SEQ, D = 2, 2048, 512
TOKENS = BATCH * SEQ
KD = D // P
INNER, NSTATE = 1024, 16
NJ = INNER // P
CTX = 77
HEADS = 16
DK = D // HEADS
FF = 2048
NF = FF // P
TC = 256
CHUNKS = TOKENS // TC
PER_BATCH = CHUNKS // BATCH
EPS = 1e-5
W_SCALE = 64.0
UNSCALE = 1.0 / W_SCALE



def split_product(nc, out, w, x, start, stop):
    nc.tensor.matmul(out, w[0], x[0], start=start, stop=False)
    nc.tensor.matmul(out, w[0], x[1], start=False, stop=False)
    return nc.tensor.matmul(out, w[1], x[0], start=False, stop=stop)


GS = 4
NG = NSTATE // GS
GROUPS = NJ * NG
DT_AT = (14, 16, 18, 20, 22, 24, 26, 27)
RING, H_RING = 4, 8


def selective_scan_phase(nc, a):
    with ExitStack() as ctx:
        def sb(name, shape, dt=FP32):
            return ctx.enter_context(nc.sbuf_tensor(name, shape, dt))

        def sem(name):
            return ctx.enter_context(nc.semaphore(name))

        half = 2 * KD * 2 * INNER
        w_in = a["region"][:, 0:half].rearrange("p (s k n) -> p s k n", s=2, k=KD)
        w_in = [w_in[:, s, :, :] for s in range(2)]
        w_dt = a["region"][:, half:2 * half].rearrange("p (s k n) -> p s k n", s=2, k=NJ)
        w_dt = [w_dt[:, s, :, :] for s in range(2)]
        w_xp = [sb(f"w_xp_{n}", [P, NJ, 2 * NSTATE], FP16) for n in ("high", "low")]
        b_in = sb("b_in", [P, 2 * NJ])
        b_dt = sb("b_dt", [P, NJ])
        b_dt64 = sb("b_dt64", [P, NJ])
        b_xp = sb("b_xp", [2 * NSTATE, 1])
        d_skip = sb("d_skip", [P, NJ])
        decay = sb("decay", [P, NJ, NSTATE])
        x_t = sb("x_t", [P, KD, TC])
        x16 = [sb(f"x_{n}", [P, 2, KD, TC], FP16) for n in ("high", "low")]
        u16 = [sb(f"u_{n}", [P, NJ, TC], FP16) for n in ("high", "low")]
        u = sb("u", [P, 2, NJ, TC])
        z = sb("z", [P, NJ, TC])
        dt = sb("dt", [P, NJ, TC])
        soft = sb("soft", [P, 4, TC])
        dtu = sb("dtu", [P, 2, TC])
        bc = sb("bc", [2 * NSTATE, TC])
        b_rep = sb("b_rep", [P, NSTATE, TC])
        c_rep = sb("c_rep", [P, NSTATE, TC])
        da = sb("da", [P, RING, GS, TC])
        h = sb("h", [P, H_RING, GS, TC])
        h_last = sb("h_last", [P, NJ, NSTATE])
        zeros = sb("zeros", [P, GS])
        y = sb("y", [P, 2, TC])

        proj = ctx.enter_context(nc.psum_tensor("proj", [P, NJ, TC], FP32))
        bc_ps = ctx.enter_context(nc.psum_tensor("bc_ps", [2 * NSTATE, 512], FP32))
        y_ps = ctx.enter_context(nc.psum_tensor("y_ps", [P, 2, 512], FP32))

        s_w = [sem(f"a_weights_{n}_loaded") for n in range(4)]
        s_wh, s_wl = sem("a_weights_high"), sem("a_weights_low")
        s_small = sem("a_small_loaded")
        s_xh, s_xl, s_uh, s_ul = sem("a_x_high"), sem("a_x_low"), sem("a_u_high"), sem("a_u_low")
        s_x = sem("a_x_loaded")
        s_const = sem("a_decay_ready")
        s_up, s_zp, s_bcp, s_dtp = sem("a_u_psum"), sem("a_z_psum"), sem("a_bc_psum"), sem("a_dt_psum")
        s_u, s_z, s_bc = sem("a_u_ready"), sem("a_z_ready"), sem("a_bc_ready")
        s_abs, s_relu = sem("a_abs_done"), sem("a_relu_done")
        s_sexp, s_soft, s_dt = sem("a_soft_exp_done"), sem("a_soft_ready"), sem("a_dt_ready")
        s_bcd = sem("a_bc_in_dram")
        s_b = [sem(f"a_b_rep_{g}") for g in range(NG)]
        s_c = [sem(f"a_c_rep_{g}") for g in range(NG)]
        s_dtu = sem("a_dtu_ready")
        s_dbu = sem("a_dbu_ready")
        s_da = sem("a_da_ready")
        s_scan = sem("a_scanned")
        s_hz, s_hl = sem("a_h_last_cleared"), sem("a_h_last_saved")
        s_hc = sem("a_hc_ready")
        s_sum = sem("a_summed")
        s_gate = sem("a_skip_added")
        s_y = sem("a_y_ready")
        s_yout = [sem("a_y_stored_even"), sem("a_y_stored_odd")]
        s_kvw, s_ones, s_kvp = sem("a_kv_weights_loaded"), sem("a_ones_ready"), sem("a_kv_psum")

        DBU_CREDIT, SCAN_CREDIT, SUM_CREDIT, GATE_CREDIT, Y_CREDIT, STORE_CREDIT = 2 * NG, RING, H_RING, 2, 1, 16

        block = ctx.enter_context(nc.Block())

        w_xp32 = c_rep[:, 0, :].rearrange("p (k n) -> p k n", k=NJ)
        pieces = []
        for n in range(4):
            stage = (h if n % 2 == 0 else da)[:, 0:4, :, :].rearrange("p r s t -> p (r s t)")
            if n < 2:
                where = (slice(None), slice(None), slice(n * INNER, (n + 1) * INNER))
                pieces.append((stage.rearrange("p (k n) -> p k n", k=KD),
                               a["w_in"].rearrange("(k p) n -> p k n", p=P)[where],
                               w_in[0][where], w_in[1][where]))
            else:
                where = (slice(None), slice((n - 2) * NJ // 2, (n - 1) * NJ // 2), slice(None))
                pieces.append((stage.rearrange("p (k n) -> p k n", k=NJ // 2),
                               a["w_dt"].rearrange("(k p) n -> p k n", p=P)[where],
                               w_dt[0][where], w_dt[1][where]))

        def all_chunks(e, main, between=None):
            half = PER_BATCH // 2
            for p in range(2):
                main(p, p, False)
            with e.Fori(1, half) as i:
                for p in range(2):
                    main(i * 2 + p, p, False)
            if between:
                between()
            with e.Fori(half, 2 * half - 1) as i:
                for p in range(2):
                    main(i * 2 + p, p, False)
            for p in range(2):
                main(CHUNKS - 2 + p, p, p == 1)

        @block.sync
        def _(sp):
            def load_x(c):
                sp.dma_start(x_t[:, :, :], a["x_t"].rearrange("(k p) t -> p k t", p=P)[:, :, bass.ds(c * TC, TC)])\
                    .then_inc(s_x, 16)

            def load_rep(rep, row, c, g, done):
                sp.dma_start(rep[:, g * GS:(g + 1) * GS, :],
                             a["bc"][bass.ds(c, 1), row + g * GS:row + (g + 1) * GS, :]
                             .broadcast_to([P, GS, TC])).then_inc(done[g], 16)

            def store_bc(c):
                sp.wait_ge(s_bc, c + 1)
                sp.dma_start(a["bc"][bass.ds(c, 1), :, :].rearrange("a s t -> (a s) t"), bc[:, :]).then_inc(s_bcd, 16)

            def load_b_rep(c, g):
                sp.wait_ge(s_dbu, c * GROUPS + 7 * NG + g + 1 + DBU_CREDIT)
                load_rep(b_rep, 0, c + 1, g, s_b)

            def load_c_rep(c, g):
                sp.wait_ge(s_hc, c * GROUPS + 7 * NG + g + 1)
                load_rep(c_rep, NSTATE, c + 1, g, s_c)

            def store_y(c, j):
                n = c * NJ + j
                sp.wait_ge(s_y, n + 1 + Y_CREDIT)
                sp.dma_start(a["y_t"][j * P:(j + 1) * P, bass.ds(c * TC, TC)], y[:, j % 2, :])\
                    .then_inc(s_yout[j % 2], 16)

            for q in range(2):
                sp.sem_inc(s_yout[q], STORE_CREDIT)
            load_x(0)
            sp.dma_start(pieces[0][0], pieces[0][1]).then_inc(s_w[0], 16)
            sp.dma_start(b_in[:, :], a["b_in"]).then_inc(s_small, 16)
            sp.dma_start(w_xp32, a["w_xproj"].rearrange("(k p) n -> p k n", p=P)).then_inc(s_small, 16)
            sp.dma_start(b_xp[:, :], a["b_xproj"]).then_inc(s_small, 16)
            sp.dma_start(decay[:, :, :], a["a_log"].rearrange("(j p) s -> p j s", p=P)).then_inc(s_small, 16)
            sp.dma_start(b_dt[:, :], a["b_dt"]).then_inc(s_small, 16)
            sp.dma_start(d_skip[:, :], a["d_param"]).then_inc(s_small, 16)
            sp.dma_start(pieces[1][0], pieces[1][1]).then_inc(s_w[1], 16)
            for n in range(2, 4):
                sp.wait_ge(s_wl, (1, 3)[n - 2])
                sp.dma_start(pieces[n][0], pieces[n][1]).then_inc(s_w[n], 16)
            sp.wait_ge(s_xl, 1)
            load_x(1)
            store_bc(0)
            sp.wait_ge(s_bcd, 16)
            for g in range(NG):
                load_rep(b_rep, 0, 0, g, s_b)
            for g in range(NG):
                load_rep(c_rep, NSTATE, 0, g, s_c)

            def main(c, p, last):
                for j in range(NJ):
                    if not last:
                        if j == 5:
                            store_bc(c + 1)
                        if j == 1 and not (isinstance(c, int) and c + 2 >= CHUNKS):
                            sp.wait_ge(s_xl, c + 2)
                            load_x(c + 2)
                    elif j == 1:
                        sp.wait_ge(s_zp, CHUNKS * NJ)
                        for dst, src in a["kv_loads"]:
                            sp.dma_start(dst, src).then_inc(s_kvw, 16)
                        for stage, src, _, _ in a["early_pieces"]:
                            sp.dma_start(stage, src).then_inc(a["s_early"], 16)
                    if not last:
                        if j == 7:
                            sp.wait_ge(s_bcd, (c + 2) * 16)
                            load_b_rep(c, 0)
                            for g in range(1, NG):
                                load_b_rep(c, g)
                                load_c_rep(c, g - 1)
                    if j > 0:
                        store_y(c, j - 1)
                    elif not (isinstance(c, int) and c == 0):
                        store_y(c - 1, NJ - 1)
                if not last:
                    load_c_rep(c, NG - 1)
                else:
                    store_y(c, NJ - 1)

            all_chunks(sp, main)
            for q in range(2):
                sp.wait_ge(s_yout[q], 16 * CHUNKS * NJ // 2 + STORE_CREDIT)

        @block.tensor
        def _(pe):
            def project(w, col, rhs, kn, dst, done, width=P):
                for k in range(kn):
                    last = split_product(nc, dst, [part[:, k, col:col + width] for part in w],
                                         [part[:, k, :] for part in rhs], k == 0, k == kn - 1)
                last.then_inc(done, 1)

            def side(c, p, j, g):
                first = isinstance(c, int) and c == 0
                x = [part[:, p, :, :] for part in x16]
                if j == 0:
                    if g == 0:
                        pe.wait_ge(s_xl, c + 1)
                        if not first:
                            pe.wait_ge(s_abs, c * NJ)
                            pe.wait_ge(s_relu, c * NJ)
                    project(w_in, g * P, x, KD, proj[:, g, :], s_up)
                if j == 1:
                    if g == 0 and not first:
                        pe.wait_ge(s_z, c * NJ)
                    project(w_in, (4 + g) * P, x, KD, proj[:, 4 + g, :], s_up)
                if j == 2:
                    if g == 0:
                        pe.wait_ge(s_u, c * NJ + 4)
                    project(w_in, INNER + g * P, x, KD, proj[:, g, :], s_zp)
                if (j, g) == (3, 1):
                    pe.wait_ge(s_ul, c * 2 + 2)
                    if not first:
                        pe.wait_ge(s_bc, c)
                    project(w_xp, 0, u16, NJ, bc_ps[:, 0:TC], s_bcp, 2 * NSTATE)
                if j * NG + g in DT_AT:
                    t = DT_AT.index(j * NG + g)
                    if t == 4:
                        pe.wait_ge(s_z, c * NJ + 4)
                    project(w_dt, t * P, u16, NJ, proj[:, (t + 4) % NJ, :], s_dtp)
                if j == 7:
                    if g == 0:
                        pe.wait_ge(s_abs, c * NJ + 4)
                        pe.wait_ge(s_relu, c * NJ + 4)
                    project(w_in, INNER + (4 + g) * P, x, KD, proj[:, 4 + g, :], s_zp)

            def sums(c, j, g):
                n = c * NJ + j
                if g == 0:
                    pe.wait_ge(s_gate, n + 1)
                pe.wait_ge(s_hc, n * NG + g + 1)
                for s in range(GS):
                    last = nc.tensor.matmul(y_ps[:, j % 2, 0:TC], a["ident"][:, :], h[:, (j * NG + g) % H_RING, s, :],
                                            start=(g == 0 and s == 0), stop=(g == NG - 1 and s == GS - 1))
                last.then_inc(s_sum, 1)

            pe.sem_inc(s_sum, SUM_CREDIT)
            for j in range(NJ):
                pe.wait_ge(s_wl, (1, 1, 3, 5, 5, 5, 5, 5)[j])
                for g in range(NG):
                    side(0, 0, j, g)
            pe.wait_ge(a["s_ident"], 2)

            def keys_values(j):
                ctx_t, wk, wv, b_v, ones = a["kv_inputs"]
                banks = proj[:, :, :].rearrange("p (b i) t -> p b (i t)", i=2)
                if j == 3:
                    pe.wait_ge(s_kvw, 16 * len(a["kv_loads"]))
                    pe.wait_ge(s_z, CHUNKS * NJ)
                    pe.wait_ge(s_abs, CHUNKS * NJ)
                    pe.wait_ge(s_relu, CHUNKS * NJ)
                    pe.wait_ge(s_ones, 1)
                    for b in range(BATCH):
                        for t in range(KD):
                            for k in range(KD):
                                last = nc.tensor.matmul(banks[:, b, t * CTX:(t + 1) * CTX], wk[:, k, t * P:(t + 1) * P],
                                                        ctx_t[:, k, b, :], start=(k == 0), stop=(k == KD - 1))
                        last.then_inc(s_kvp, 1)
                if j in (4, 5):
                    b = j - 4
                    for k in range(KD):
                        nc.tensor.matmul(banks[0:CTX, BATCH + b, :], ctx_t[:, k, b, :], wv[:, k, :], start=(k == 0), stop=False)
                    nc.tensor.matmul(banks[0:CTX, BATCH + b, :], ones, b_v, start=False, stop=True).then_inc(s_kvp, 1)

            def main(c, p, last):
                for j in range(NJ):
                    for g in range(NG):
                        if not last:
                            side(c + 1, 1 - p, j, g)
                        elif g == 0:
                            keys_values(j)
                        sums(c, j, g)

            all_chunks(pe, main)

        @block.scalar
        def _(act):
            def silu(c, t, dst, col, psum_sem, done):
                act.wait_ge(psum_sem, c * NJ + t // 2 * 2 + 2)
                nc.scalar.activation(dst, proj[:, t, :], ACT.Silu, bias=b_in[:, col:col + 1], scale=UNSCALE)\
                    .then_inc(done, 1)

            def silu_u(c, p, t):
                silu(c, t, u[:, p, t, :], t, s_up, s_u)

            def u_high(c, p, half):
                tiles = slice(4 * half, 4 * half + 4)
                act.wait_ge(s_u, c * NJ + 4 * half + 4)
                nc.scalar.activation(u16[0][:, tiles, :], u[:, p, tiles, :], ACT.Copy).then_inc(s_uh, 1)

            def x_high(c, p):
                act.wait_ge(s_x, (c + 1) * 16)
                nc.scalar.activation(x16[0][:, p, :, :], x_t[:, :, :], ACT.Copy).then_inc(s_xh, 1)

            def silu_z(c, t):
                silu(c, t, z[:, t, :], NJ + t, s_zp, s_z)

            def evacuate_bc(c):
                act.wait_ge(s_bcp, c + 1)
                if not (isinstance(c, int) and c == 0):
                    act.wait_ge(s_bcd, c * 16)
                nc.scalar.activation(bc[:, :], bc_ps[:, 0:TC], ACT.Identity, bias=b_xp[:, 0:1], scale=UNSCALE)\
                    .then_inc(s_bc, 1)

            def soft_exp(c, t0):
                s0 = t0 % 4
                for t in range(t0, t0 + 2):
                    slot = t + 4 if t < 4 else t - 4
                    act.wait_ge(s_dtp, c * NJ + t // 2 * 2 + 2)
                    nc.scalar.activation(soft[:, t % 4, :], proj[:, slot, :], ACT.Abs, bias=b_dt[:, t:t + 1],
                                         scale=UNSCALE).then_inc(s_abs, 1)
                act.wait_ge(s_abs, c * NJ + t0 + 2)
                nc.scalar.activation(soft[:, s0:s0 + 2, :], soft[:, s0:s0 + 2, :], ACT.Exp, scale=-1.0).then_inc(s_sexp, 1)

            def soft_ln(c, half):
                act.wait_ge(s_sexp, c * 4 + 2 * half + 2)
                nc.scalar.activation(soft[:, :, :], soft[:, :, :], ACT.Ln, bias=1.0).then_inc(s_soft, 1)

            def weights_high(n):
                act.wait_ge(s_w[n], 16)
                nc.scalar.activation(pieces[n][2], pieces[n][0], ACT.Copy, scale=W_SCALE).then_inc(s_wh, 1)

            x_high(0, 0)
            weights_high(0)
            act.wait_ge(s_small, 96)
            nc.scalar.activation(w_xp[0][:, :, :], w_xp32, ACT.Copy, scale=W_SCALE).then_inc(s_wh, 1)
            nc.scalar.activation(decay[:, :, :], decay[:, :, :], ACT.Exp).then_inc(s_const, 1)
            weights_high(1)
            for half in range(2):
                for t in range(4 * half, 4 * half + 4):
                    silu_u(0, 0, t)
                u_high(0, 0, half)
                weights_high(2 + half)
            for t in range(4):
                silu_z(0, t)
            evacuate_bc(0)
            soft_exp(0, 0)
            soft_exp(0, 2)
            soft_ln(0, 0)
            act.wait_ge(s_dt, 1)
            soft_exp(0, 4)
            act.wait_ge(s_const, 2)
            x_high(1, 1)

            def side(c, p, g, last):
                if g == 0:
                    soft_exp(c, 6)
                    soft_ln(c, 1)
                if g == 7:
                    act.wait_ge(s_y, c * NJ + Y_CREDIT)
                    for t in range(4, 8):
                        silu_z(c, t)
                if last:
                    banks = proj[:, :, :].rearrange("p (b i) t -> p b (i t)", i=2)
                    if g in (18, 19):
                        b = g - 18
                        act.wait_ge(s_kvp, b + 1)
                        for t in range(KD):
                            nc.scalar.activation(a["k_t"][:, b, t, :], banks[:, b, t * CTX:(t + 1) * CTX], ACT.Identity,
                                                 bias=a["b_k"][:, t:t + 1])
                    if g in (26, 30):
                        b = (g - 26) // 4
                        act.wait_ge(s_kvp, BATCH + b + 1)
                        nc.scalar.activation(a["v"][:, b, :], banks[0:CTX, BATCH + b, :], ACT.Copy)
                    return
                if g == 9:
                    act.wait_ge(s_gate, c * NJ + GATE_CREDIT)
                    for t in range(4):
                        silu_u(c + 1, 1 - p, t)
                    u_high(c + 1, 1 - p, 0)
                if g == 13:
                    for t in range(4, 8):
                        silu_u(c + 1, 1 - p, t)
                    u_high(c + 1, 1 - p, 1)
                if g == 16 and not (isinstance(c, int) and c + 2 >= CHUNKS):
                    act.wait_ge(s_zp, (c + 1) * NJ)
                    x_high(c + 2, p)
                if g == 18:
                    evacuate_bc(c + 1)
                if g == 21:
                    act.wait_ge(s_dt, c * 2 + 2)
                    soft_exp(c + 1, 0)
                if g == 23:
                    act.wait_ge(s_y, c * NJ + 4 + Y_CREDIT)
                    for t in range(4):
                        silu_z(c + 1, t)
                if g == 25:
                    soft_exp(c + 1, 2)
                    soft_ln(c + 1, 0)
                if g == 29:
                    act.wait_ge(s_dt, (c + 1) * 2 + 1)
                    soft_exp(c + 1, 4)

            def main(c, p, last):
                for g in range(GROUPS):
                    j = g // NG
                    if g in (0, GROUPS // 2):
                        act.wait_ge(s_dt, c * 2 + 1 + 2 * g // GROUPS)
                    act.wait_ge(s_scan, c * GROUPS + g + 1)
                    for s in range(GS):
                        st = g % NG * GS + s
                        last_exp = nc.scalar.activation(da[:, g % RING, s, :], dt[:, j, :], ACT.Exp,
                                                        scale=decay[:, j, st:st + 1])
                    last_exp.then_inc(s_da, 1)
                    side(c, p, g, last)

            all_chunks(act, main)

        @block.vector
        def _(dve):
            def relu(c, t0, t1, after_scan):
                for t in range(t0, t1):
                    slot = t + 4 if t < 4 else t - 4
                    dve.wait_ge(s_abs, c * NJ + t // 2 * 2 + 2)
                    if after_scan:
                        dve.wait_ge(s_da, (c - 1) * GROUPS + (t + 1) * NG)
                        dve.wait_ge(s_dtu, (c - 1) * NJ + t + 1)
                    nc.vector.tensor_scalar(dt[:, t, :], proj[:, slot, :], b_dt64[:, t:t + 1], 0.0, ALU.add, ALU.max)\
                        .then_inc(s_relu, 1)

            def add_soft(c, half):
                tiles = slice(4 * half, 4 * half + 4)
                dve.wait_ge(s_soft, c * 2 + half + 1)
                dve.wait_ge(s_relu, c * NJ + 4 * half + 4)
                nc.vector.scalar_tensor_tensor(dt[:, tiles, :], dt[:, tiles, :], UNSCALE, soft[:, :, :],
                                               ALU.mult, ALU.add).then_inc(s_dt, 1)

            def weights_low(high, stage, low, n):
                dve.wait_ge(s_wh, n + 1)
                nc.vector.scalar_tensor_tensor(low, stage, W_SCALE, high, ALU.mult, ALU.subtract).then_inc(s_wl, 1)

            def dbu(c, p, j, g):
                m = c * GROUPS + j * NG + g
                if g == 0:
                    dve.wait_ge(s_dtu, c * NJ + j + 1)
                if j == 0:
                    dve.wait_ge(s_b[g], (c + 1) * 16)
                dve.wait_ge(s_sum, m + 1)
                nc.vector.tensor_tensor(h[:, (j * NG + g) % H_RING, :, :],
                                        dtu[:, j % 2:j % 2 + 1, :].broadcast_to([P, GS, TC]),
                                        b_rep[:, g * GS:(g + 1) * GS, :], ALU.mult).then_inc(s_dbu, 1)

            def scans(c, j, g):
                m = c * GROUPS + j * NG + g
                r, r_h = (j * NG + g) % RING, (j * NG + g) % H_RING
                dve.wait_ge(s_da, m + 1)
                dve.wait_ge(s_dbu, m + 1 + DBU_CREDIT)
                dve.wait_ge(s_hl, m + 1)
                for s in range(GS):
                    st = g * GS + s
                    last = nc.vector.tensor_tensor_scan(h[:, r_h, s, :], da[:, r, s, :], h[:, r_h, s, :],
                                                        h_last[:, j, st:st + 1], ALU.mult, ALU.add)
                last.then_inc(s_scan, 1)

            def gate(c, p, j):
                n = c * NJ + j
                dve.wait_ge(s_sum, (n + 1) * NG + SUM_CREDIT)
                dve.wait_ge(s_yout[j % 2], (c * (NJ // 2) + j // 2) * 16 + STORE_CREDIT)
                nc.vector.scalar_tensor_tensor(y[:, j % 2, :], u[:, p, j, :], d_skip[:, j:j + 1], y_ps[:, j % 2, 0:TC],
                                               ALU.mult, ALU.add).then_inc(s_gate, 1)

            dve.sem_inc(s_dbu, DBU_CREDIT)
            dve.sem_inc(s_scan, SCAN_CREDIT)
            dve.sem_inc(s_gate, GATE_CREDIT)
            weights_low(pieces[0][2], pieces[0][0], pieces[0][3], 0)
            weights_low(w_xp[0][:, :, :], w_xp32, w_xp[1][:, :, :], 1)
            dve.wait_ge(s_const, 1)
            nc.vector.tensor_scalar(decay[:, :, :], decay[:, :, :], -1.0, None, ALU.mult).then_inc(s_const, 1)
            nc.vector.tensor_scalar(b_dt64[:, :], b_dt[:, :], W_SCALE, None, ALU.mult).then_inc(s_const, 1)
            for n in range(1, 4):
                weights_low(pieces[n][2], pieces[n][0], pieces[n][3], n + 1)
            dve.wait_ge(s_const, 3)
            relu(0, 0, 4, False)
            add_soft(0, 0)
            relu(0, 4, 8, False)
            dbu(0, 0, 0, 0)
            dve.wait_ge(s_hz, 2)

            def main(c, p, last):
                for j in range(NJ):
                    for g in range(NG):
                        if g < NG - 1:
                            dbu(c, p, j, g + 1)
                        elif j < NJ - 1:
                            dbu(c, p, j + 1, 0)
                        elif not last:
                            dbu(c + 1, 1 - p, 0, 0)
                        scans(c, j, g)
                        if g == 3:
                            if j > 0:
                                gate(c, p, j - 1)
                            elif not (isinstance(c, int) and c == 0):
                                gate(c - 1, 1 - p, NJ - 1)
                        if g == 2 and j == 0:
                            add_soft(c, 1)
                        if last:
                            continue
                        if j * NG + g in (20, 24, 28, 31):
                            t = 2 * (20, 24, 28, 31).index(j * NG + g)
                            relu(c + 1, t, t + 2, True)
                        if j * NG + g == 25:
                            add_soft(c + 1, 0)
                if last:
                    gate(c, p, NJ - 1)

            all_chunks(dve, main, lambda: dve.wait_ge(s_hz, 3))

        @block.gpsimd
        def _(pool):
            def dt_times_u(c, p, j):
                n = c * NJ + j
                if j in (0, 4):
                    pool.wait_ge(s_dt, c * 2 + 1 + j // 4)
                pool.wait_ge(s_u, n + 1)
                pool.wait_ge(s_dbu, n * NG + NG)
                nc.gpsimd.tensor_tensor(dtu[:, j % 2, :], dt[:, j, :], u[:, p, j, :], ALU.mult).then_inc(s_dtu, 1)

            def finish_y(c, p, j):
                n = c * NJ + j
                pool.wait_ge(s_gate, n + 1 + GATE_CREDIT)
                pool.wait_ge(s_z, n + 1)
                nc.gpsimd.tensor_tensor(y[:, j % 2, :], y[:, j % 2, :], z[:, j, :], ALU.mult).then_inc(s_y, 1)

            def x_low(c, p):
                pool.wait_ge(s_xh, c + 1)
                nc.gpsimd.tensor_tensor(x16[1][:, p, :, :], x_t[:, :, :], x16[0][:, p, :, :], ALU.subtract).then_inc(s_xl, 1)

            def u_low(c, p, half):
                tiles = slice(4 * half, 4 * half + 4)
                pool.wait_ge(s_uh, c * 2 + half + 1)
                nc.gpsimd.tensor_tensor(u16[1][:, tiles, :], u[:, p, tiles, :], u16[0][:, tiles, :], ALU.subtract)\
                    .then_inc(s_ul, 1)

            def clear_h_last():
                nc.gpsimd.memset(h_last[:, :, :], 0.0).then_inc(s_hz, 1)

            pool.sem_inc(s_y, Y_CREDIT)
            pool.sem_inc(s_hl, GROUPS)
            nc.gpsimd.memset(a["ident"][:, :], 0.0).then_inc(a["s_ident"], 1)
            pool.wait_ge(a["s_ident"], 1)
            nc.gpsimd.affine_select(out=a["ident"][:, :], in_=a["ident"][:, :], compare_op=ALU.not_equal, fill=1.0,
                                    base=0, pattern=[[-1, P]], channel_multiplier=1).then_inc(a["s_ident"], 1)
            nc.gpsimd.memset(zeros[:, :], 0.0).then_inc(s_hz, 1)
            clear_h_last()
            x_low(0, 0)
            u_low(0, 0, 0)
            u_low(0, 0, 1)
            pool.wait_ge(s_hz, 2)
            x_low(1, 1)
            dt_times_u(0, 0, 0)

            def main(c, p, last):
                for j in range(NJ):
                    for g in range(NG):
                        m = c * GROUPS + j * NG + g
                        r = (j * NG + g) % H_RING
                        pool.wait_ge(s_scan, m + 1 + SCAN_CREDIT)
                        nc.gpsimd.tensor_tensor(h_last[:, j, g * GS:(g + 1) * GS], h[:, r, :, TC - 1], zeros[:, :],
                                                ALU.add).then_inc(s_hl, 1)
                        if last and (j, g) == (1, 0):
                            pool.wait_ge(s_zp, CHUNKS * NJ)
                            nc.gpsimd.memset(a["kv_inputs"][-1], 1.0).then_inc(s_ones, 1)
                        if j == 0:
                            pool.wait_ge(s_c[g], (c + 1) * 16)
                        pool.wait_ge(s_hl, m + 1 + GROUPS)
                        nc.gpsimd.tensor_tensor(h[:, r, :, :], h[:, r, :, :], c_rep[:, g * GS:(g + 1) * GS, :], ALU.mult)\
                            .then_inc(s_hc, 1)
                        if g == 0:
                            if j < NJ - 1:
                                dt_times_u(c, p, j + 1)
                            elif not last:
                                dt_times_u(c + 1, 1 - p, 0)
                        if not last and j * NG + g in (8, 12):
                            u_low(c + 1, 1 - p, (8, 12).index(j * NG + g))
                        if not last and j * NG + g == 20 and not (isinstance(c, int) and c + 2 >= CHUNKS):
                            x_low(c + 2, p)
                        if g == 3:
                            if j > 0:
                                finish_y(c, p, j - 1)
                            elif not (isinstance(c, int) and c == 0):
                                finish_y(c - 1, 1 - p, NJ - 1)
                if last:
                    finish_y(c, p, NJ - 1)

            def between():
                pool.wait_ge(s_hl, (PER_BATCH + 1) * GROUPS)
                clear_h_last()

            all_chunks(pool, main, between)


LANES = P // DK
HU = HEADS // LANES
NT = TC // P
NU = NF // 2
TWO_PI = 2.0 * math.pi
ROUND = 1.5 * 2.0 ** 23
MASKED = 1.0e9


def attention_ffn_phase(nc, a):
    with ExitStack() as ctx:
        def sb(name, shape, dt=FP32):
            return ctx.enter_context(nc.sbuf_tensor(name, shape, dt))

        def ps(name, shape):
            return ctx.enter_context(nc.psum_tensor(name, shape, FP32))

        def sem(name):
            return ctx.enter_context(nc.semaphore(name))

        ident = a["ident"]
        w_out = sb("w_out", [P, 2, NJ, D], FP16)
        w_q = sb("w_q", [P, 2, KD, D], FP16)
        w_o = sb("w_o", [P, 2, KD, D], FP16)
        k_t = sb("k_t", [P, BATCH, KD, CTX])
        v = sb("v", [CTX, BATCH, D])
        w_1, w_2 = a["w_1_split"], a["w_2_split"]
        rows = sb("rows", [P, 3, D])
        b_q = sb("b_q", [P, KD])
        b_1 = sb("b_1", [P, NF])
        theta = sb("theta", [P, NF])
        w_re = sb("w_re", [P, NF])
        w_im = sb("w_im", [P, NF])
        turns = sb("turns", [P, NF])
        gain = sb("gain", [P, NF])
        tmp = sb("tmp", [P, 3, NF])
        eps = sb("eps", [P, 1])
        y_t = sb("y_t", [P, NJ, TC])
        y16 = sb("y16", [P, 2, NJ, TC], FP16)
        x_in = sb("x_in", [P, NT, D])
        x1 = sb("x1", [P, NT, D])
        x2 = sb("x2", [P, NT, D])
        x3 = sb("x3", [P, NT, D])
        xa16 = sb("xa16", [P, 2, KD, TC], FP16)
        q_t = sb("q_t", [P, KD, TC])
        x2_16 = sb("x2_16", [P, 2, KD, TC], FP16)
        stats = sb("stats", [P, 3, NT, 6])
        mv = sb("mv", [P, 3, NT, 2])
        std = sb("std", [P, 3, NT])
        rstd = sb("rstd", [P, 3, NT])
        mask_i = sb("mask_i", [P, NT, CTX], INT32)
        keep = sb("keep", [P, NT, CTX])
        fill = sb("fill", [P, NT, CTX])
        pr = sb("pr", [P, NT, HEADS, CTX])
        smax = sb("smax", [P, NT, HEADS])
        ssum = sb("ssum", [P, NT, HEADS])
        sinv = sb("sinv", [P, NT, HEADS])
        p_t = sb("p_t", [P, HEADS, P])
        act16 = sb("act16", [P, 2, NF, TC], FP16)
        units = sb("units", [P, 8, 2, TC])
        hid = units[:, 0:3, :, :]
        arg = units[:, 3:6, :, :]
        whole = units[:, 6:8, :, :]

        nat = ps("nat", [P, 2, D])
        tr = ps("tr", [P, KD, TC])
        fps = ps("fps", [P, 2, 2, TC])
        sps = ps("sps", [P, 2, 512])
        act_parts = [act16[:, n, :, :].rearrange("p f t -> p (f t)").bitcast(FP32) for n in range(2)]
        unit_parts = [units[:, 4 * n:4 * n + 4, :, :].rearrange("p u i t -> p (u i t)") for n in range(2)]
        stages = act_parts + unit_parts
        pieces = [(stage, src, split_of[:, 0, k:k + 4, :], split_of[:, 1, k:k + 4, :]) for (stage, src, _, _), (split_of, k)
                  in zip(a["early_pieces"], ((w_out, 0), (w_out, 4), (w_q, 0), (w_o, 0)))]
        for name, w, k_step in (("w_1", w_1, 1), ("w_2", w_2, 4)):
            for k in range(0, w.shape[2], k_step):
                stage = stages[len(pieces) % 4].rearrange("p (k n) -> p k n", k=k_step)
                pieces.append((stage, a[name].rearrange("(k p) n -> p k n", p=P)[:, k:k + k_step, :],
                               w[:, 0, k:k + k_step, :], w[:, 1, k:k + k_step, :]))
        OUT_SPLIT, Q_O_SPLIT, W1_SPLIT, W2_SPLIT = 2, 4, 8, 12

        s_kv = sem("b_keys_values_moved")
        s_stage = [sem(f"b_piece_loaded_{n}") for n in range(4)]
        s_whi, s_wlo = sem("b_weights_high"), sem("b_weights_low")
        s_yh, s_yl = sem("b_y_high"), sem("b_y_low")
        s_small, s_rows = sem("b_small_loaded"), sem("b_rows_loaded")
        s_yt, s_xin, s_mask = sem("b_yt_loaded"), sem("b_x_loaded"), sem("b_mask_loaded")
        s_out = sem("b_out_stored")
        s_chain, s_ss, s_tick = sem("b_param_chain"), sem("b_softmax_sums"), sem("b_statistics_awaited")
        s_par, s_parv = sem("b_param_act"), sem("b_param_dve")
        s_nat = {n: sem(f"b_{n}_psum") for n in ("outproj", "wo", "w2")}
        s_r = {n: sem(f"b_{n}_residual") for n in ("outproj", "wo", "w2")}
        s_st, s_mv, s_sd, s_rs, s_x = ({n: sem(f"b_{n}_{w}") for n in ("outproj", "wo", "w2")}
                                       for w in ("stats", "meanvar", "std", "rstd", "normed"))
        s_xb = {n: sem(f"b_{n}_bias_added") for n in ("xin", "outproj", "wo")}
        s_x1tp, s_x1t, s_qp, s_q = sem("b_x1t_psum"), sem("b_x1t"), sem("b_q_psum"), sem("b_q")
        s_x2tp, s_x2t = sem("b_x2t_psum"), sem("b_x2t")
        s_x1l, s_x2l, s_avl, s_actl = (sem(f"b_{n}_low") for n in ("x1t", "x2t", "av", "act"))
        s_keep = sem("b_keep_ready")
        s_scp, s_sc = sem("b_scores_psum"), sem("b_scores_read")
        s_sma, s_smb = sem("b_scores_less_maximum"), sem("b_sums_inverse")
        s_pexp, s_pn = sem("b_exp_done"), sem("b_probs_ready")
        s_ptp, s_pt = sem("b_pt_psum"), sem("b_pt")
        s_avp, s_av = sem("b_av_psum"), sem("b_av")
        s_hp, s_h, s_arg, s_wh, s_fr, s_sin, s_mix, s_act = (sem(f"b_ffn_{n}") for n in (
            "psum", "hidden", "argument", "whole", "fraction", "sine", "mixed", "act"))

        block = ctx.enter_context(nc.Block())

        def all_chunks(e, front_back):
            front_back(0, 0, True, False)
            front_back(1, 0, True, True)
            with e.Fori(2, PER_BATCH) as c:
                front_back(c, 0, True, True)
            with e.Fori(PER_BATCH, CHUNKS - 1) as c:
                front_back(c, 1, True, True)
            front_back(CHUNKS - 1, 1, True, True)
            front_back(CHUNKS, 1, False, True)

        @block.sync
        def _(sp):
            def load(dst, src, s):
                sp.dma_start(dst, src).then_inc(s, 16)

            def load_mask(c, batch):
                load(mask_i[:, :, :], a["mask"].rearrange("(t p) s -> p t s", p=P)
                     [:, bass.ds((c - batch * PER_BATCH) * NT, NT), :], s_mask)

            def load_y(c):
                sp.wait_ge(s_yl, c)
                load(y_t[:, :, :], a["y_t"].rearrange("(j p) t -> p j t", p=P)[:, :, bass.ds(c * TC, TC)], s_yt)

            load(y_t[:, :, :], a["y_t"].rearrange("(j p) t -> p j t", p=P)[:, :, 0:TC], s_yt)
            load(x_in[:, :, :], a["x"].rearrange("(t p) d -> p t d", p=P)[:, 0:NT, :], s_xin)
            for n, name in enumerate(("b_out", "b_o", "b_2")):
                load(rows[:, n, :], a[name].broadcast_to([P, D]), s_rows)
            for dst, name in ((b_q, "b_q"), (b_1, "b_1"), (theta, "theta"), (w_re, "w_re"), (w_im, "w_im")):
                load(dst[:, :], a[name], s_small)
            load_mask(0, 0)
            for n in range(4, 8):
                load(pieces[n][0], pieces[n][1], s_stage[n % 4])
            load_y(1)
            for n in range(8, len(pieces)):
                sp.wait_ge(s_wlo, n - 3)
                load(pieces[n][0], pieces[n][1], s_stage[n % 4])

            def front_back(c, batch, front, back):
                if front and back:
                    sp.wait_ge(s_keep, c * 2)
                    load_mask(c, batch)
                if front and not (isinstance(c, int) and c == CHUNKS - 1):
                    if back:
                        load_y(c + 1)
                    sp.wait_ge(s_r["outproj"], (c + 1) * NT)
                    load(x_in[:, :, :], a["x"].rearrange("(t p) d -> p t d", p=P)[:, bass.ds((c + 1) * NT, NT), :], s_xin)
                if back:
                    sp.wait_ge(s_x["w2"], c * NT)
                    load(a["out"].rearrange("(t p) d -> p t d", p=P)[:, bass.ds((c - 1) * NT, NT), :], x3[:, :, :], s_out)

            all_chunks(sp, front_back)
            sp.wait_ge(s_out, CHUNKS * 16)

        @block.tensor
        def _(pe):
            mm = nc.tensor.matmul
            def transposes(src, dst, done):
                for t in range(NT):
                    for k in range(KD):
                        last = nc.tensor.transpose(dst[:, k, t * P:(t + 1) * P], src[:, t, k * P:(k + 1) * P], ident[:, :])
                last.then_inc(done, 1)

            def natural(lhs, w, kn, t, k0, k1, done):
                for k in range(k0, k1):
                    last = split_product(nc, nat[:, t, :], [lhs[:, s, k, t * P:(t + 1) * P] for s in range(2)],
                                         [w[:, s, k, :] for s in range(2)], k == 0, k == kn - 1)
                if k1 == kn:
                    last.then_inc(done, 1)

            def hidden(b, n):
                if n == 0:
                    pe.wait_ge(s_x2l, b + 1)
                pe.wait_ge(s_h, b * NU + max(n - 1, 0))
                for i in range(2):
                    f = 2 * n + i
                    for k in range(KD):
                        last = split_product(nc, fps[:, n % 2, i, :], [w_1[:, s, k, f * P:(f + 1) * P] for s in range(2)],
                                             [x2_16[:, s, k, :] for s in range(2)], k == 0, k == KD - 1)
                    last.then_inc(s_hp, 1)

            def scores(c, t, batch, lanes):
                for lane in lanes:
                    unit = t * LANES + lane
                    if unit < 2:
                        pe.wait_ge(s_pt, c * 8)
                    else:
                        pe.wait_ge(s_sc, c * 8 + unit - 1)
                    rows_of = slice(lane * DK, (lane + 1) * DK)
                    for i in range(HU):
                        last = mm(sps[:, unit % 2, i * CTX:(i + 1) * CTX],
                                  q_t[rows_of, i, t * P:(t + 1) * P], k_t[rows_of, batch, i, :],
                                  start=True, stop=True)
                    last.then_inc(s_scp, 1)

            def probs_t(c, t, quarters):
                pe.wait_ge(s_pn, c * NT + t + 1)
                for n in quarters:
                    unit = t * 4 + n
                    if unit < 2:
                        pe.wait_ge(s_sc, c * 8 + 8)
                    else:
                        pe.wait_ge(s_pt, c * 8 + unit - 1)
                    for i in range(4):
                        last = nc.tensor.transpose(sps[0:CTX, unit % 2, i * P:(i + 1) * P], pr[:, t, 4 * n + i, :], ident[:, :])
                    last.then_inc(s_ptp, 1)

            def second(b, t, n0, n1):
                for n in range(n0, n1):
                    pe.wait_ge(s_actl, b * NU + n + 1)
                    natural(act16, w_2, NF, t, 2 * n, 2 * n + 2, s_nat["w2"])

            def attend(c, t, batch):
                pe.wait_ge(s_pt, c * 8 + 4 * t + 4)
                for hh in range(HEADS):
                    r = DK * (hh % LANES)
                    last = mm(tr[r:r + DK, hh // LANES, t * P:(t + 1) * P], v[:, batch, hh * DK:(hh + 1) * DK],
                              p_t[0:CTX, HU * (hh % LANES) + hh // LANES, :], start=True, stop=True)
                last.then_inc(s_avp, 1)

            def front_back(c, batch, front, back):
                b = c - 1
                if front:
                    pe.wait_ge(s_wlo, OUT_SPLIT)
                    pe.wait_ge(s_yl, c + 1)
                    pe.wait_ge(s_r["wo"], c * NT)
                    natural(y16, w_out, NJ, 0, 0, NJ, s_nat["outproj"])
                if back:
                    pe.wait_ge(s_x["wo"], c * NT)
                    pe.wait_ge(s_avl, c)
                    transposes(x2, tr, s_x2tp)
                if front:
                    natural(y16, w_out, NJ, 1, 0, NJ, s_nat["outproj"])
                if back:
                    pe.wait_ge(s_wlo, W1_SPLIT)
                    for n in range(4):
                        hidden(b, n)
                if front:
                    pe.wait_ge(s_x["outproj"], (c + 1) * NT)
                    pe.wait_ge(s_x2l, c)
                    transposes(x1, tr, s_x1tp)
                if back:
                    hidden(b, 4)
                    hidden(b, 5)
                if front:
                    pe.wait_ge(s_wlo, Q_O_SPLIT)
                    pe.wait_ge(s_x1l, c + 1)
                    for t in range(KD):
                        for k in range(KD):
                            last = split_product(nc, tr[:, t, :], [w_q[:, s, k, t * P:(t + 1) * P] for s in range(2)],
                                                 [xa16[:, s, k, :] for s in range(2)], k == 0, k == KD - 1)
                        last.then_inc(s_qp, 1)
                if back:
                    hidden(b, 6)
                if front:
                    pe.wait_ge(s_q, (c + 1) * KD)
                    scores(c, 0, batch, (0, 1))
                if back:
                    hidden(b, 7)
                if front:
                    scores(c, 0, batch, (2, 3))
                if back:
                    pe.wait_ge(s_wlo, W2_SPLIT)
                    if front:
                        pe.wait_ge(s_r["outproj"], (c + 1) * NT)
                    else:
                        pe.wait_ge(s_r["wo"], c * NT)
                    second(b, 0, 0, 3)
                if front:
                    scores(c, 1, batch, (0, 1))
                if back:
                    second(b, 0, 3, 5)
                if front:
                    scores(c, 1, batch, (2, 3))
                if back:
                    second(b, 0, 5, 8)
                    second(b, 1, 0, 2)
                for t in range(NT):
                    for half in range(2):
                        if front:
                            probs_t(c, t, (2 * half, 2 * half + 1))
                        if back:
                            second(b, 1, 2 + 2 * t + half, 3 + 2 * t + half)
                    if front:
                        attend(c, t, batch)
                if back:
                    second(b, 1, 6, 8)
                if front:
                    pe.wait_ge(s_avl, c + 1)
                    for t in range(NT):
                        if back:
                            pe.wait_ge(s_r["w2"], b * NT + t + 1)
                        else:
                            pe.wait_ge(s_r["outproj"], (c + 1) * NT)
                        natural(xa16, w_o, KD, t, 0, KD, s_nat["wo"])

            pe.wait_ge(s_kv, 2)
            all_chunks(pe, front_back)

        @block.scalar
        def _(act):
            def weights_high(n):
                if n < 4:
                    act.wait_ge(a["s_early"], 4 * 16)
                else:
                    act.wait_ge(s_stage[n % 4], 16 * (n // 4))
                nc.scalar.activation(pieces[n][2], pieces[n][0], ACT.Copy, scale=W_SCALE).then_inc(s_whi, 1)

            def y_high(c):
                act.wait_ge(s_yt, (c + 1) * 16)
                nc.scalar.activation(y16[:, 0, :, :], y_t[:, :, :], ACT.Copy).then_inc(s_yh, 1)

            weights_high(0)
            y_high(0)
            weights_high(1)
            nc.scalar.activation(k_t[:, :, :, :], a["k_t"], ACT.Copy).then_inc(s_kv, 1)
            nc.scalar.activation(v[:, :, :], a["v"], ACT.Copy).then_inc(s_kv, 1)
            act.wait_ge(s_small, 5 * 16)
            act.wait_ge(s_parv, 1)
            nc.scalar.activation(tmp[:, 0:2, :], tmp[:, 0:2, :], ACT.Sin, scale=6.283185).then_inc(s_par, 1)
            weights_high(2)
            weights_high(3)
            act.wait_ge(s_parv, 2)

            def deviation(n, i, c):
                act.wait_ge(s_mv[n], c + 1)
                nc.scalar.activation(std[:, i, :], mv[:, i, :, 1], ACT.Sqrt, bias=eps[:, 0:1]).then_inc(s_sd[n], 1)

            def hid_out(b, n):
                act.wait_ge(s_actl, b * NU + max(n - 2, 0))
                act.wait_ge(s_hp, b * NF + 2 * n + 2)
                for i in range(2):
                    f = 2 * n + i
                    nc.scalar.activation(arg[:, n % 3, i, :], fps[:, n % 2, i, :], ACT.Identity,
                                         bias=turns[:, f:f + 1], scale=UNSCALE * 0.1 / TWO_PI)
                for i in range(2):
                    f = 2 * n + i
                    last = nc.scalar.activation(hid[:, n % 3, i, :], fps[:, n % 2, i, :], ACT.Identity,
                                                bias=b_1[:, f:f + 1], scale=UNSCALE)
                last.then_inc(s_h, 1)

            def sine(b, n):
                act.wait_ge(s_fr, b * NU + n + 1)
                nc.scalar.activation(arg[:, n % 3, :, :], arg[:, n % 3, :, :], ACT.Sin, scale=6.283185).then_inc(s_sin, 1)

            def relu(b, n):
                act.wait_ge(s_mix, b * NF + 2 * n + 2)
                if n == 0:
                    act.wait_ge(s_nat["w2"], b * NT)
                nc.scalar.activation(act16[:, 0, 2 * n:2 * n + 2, :], hid[:, n % 3, :, :], ACT.Relu).then_inc(s_act, 1)

            def exps(c, t):
                act.wait_ge(s_sma, (c * NT + t) * 3 + 3)
                nc.scalar.activation(pr[:, t, :, :], pr[:, t, :, :], ACT.Exp).then_inc(s_pexp, 1)

            def probs_out(c, t):
                for n in range(4):
                    act.wait_ge(s_ptp, c * 8 + t * 4 + n + 1)
                    if n == 0:
                        act.wait_ge(s_avp, c * NT + t)
                    nc.scalar.activation(p_t[0:CTX, 4 * n:4 * n + 4, :],
                                         sps[0:CTX, n % 2, :].rearrange("p (h t) -> p h t", h=4), ACT.Copy).then_inc(s_pt, 1)

            def front_back(c, batch, front, back):
                b = c - 1
                if back:
                    act.wait_ge(s_x2tp, c)
                    act.wait_ge(s_hp, b * NF)
                    nc.scalar.activation(x2_16[:, 0, :, :], tr[:, :, :], ACT.Copy).then_inc(s_x2t, 1)
                if front:
                    deviation("outproj", 0, c)
                if not back:
                    weights_high(4)
                    weights_high(5)
                if back:
                    for n in range(4):
                        hid_out(b, n)
                        if n >= 1:
                            sine(b, n - 1)
                        if n >= 2:
                            relu(b, n - 2)
                if front:
                    act.wait_ge(s_x1tp, c + 1)
                    act.wait_ge(s_nat["wo"], c * NT)
                    nc.scalar.activation(xa16[:, 0, :, :], tr[:, :, :], ACT.Copy).then_inc(s_x1t, 1)
                if not back:
                    weights_high(6)
                if back:
                    for n in range(4, 6):
                        hid_out(b, n)
                        sine(b, n - 1)
                        relu(b, n - 2)
                if front:
                    for t in range(KD):
                        act.wait_ge(s_qp, c * KD + t // 2 * 2 + 2)
                        if t == 0:
                            act.wait_ge(s_scp, c * 8)
                        nc.scalar.activation(q_t[:, t, :], tr[:, t, :], ACT.Identity, bias=b_q[:, t:t + 1],
                                             scale=UNSCALE * DK ** -0.5).then_inc(s_q, 1)
                if not back:
                    weights_high(7)
                if back:
                    for n in range(6, 8):
                        hid_out(b, n)
                        sine(b, n - 1)
                        relu(b, n - 2)
                    sine(b, 7)
                    relu(b, 6)
                    relu(b, 7)
                if front and not (isinstance(c, int) and c == CHUNKS - 1):
                    act.wait_ge(s_nat["outproj"], (c + 1) * NT)
                    y_high(c + 1)
                for t in range(NT):
                    if front:
                        exps(c, t)
                    if not back:
                        weights_high(8 + t)
                for t in range(NT):
                    if front:
                        probs_out(c, t)
                    if not back and t == 0:
                        weights_high(10)
                if front:
                    act.wait_ge(s_avp, (c + 1) * NT)
                    act.wait_ge(s_qp, (c + 1) * KD)
                    nc.scalar.activation(xa16[:, 0, :, :], tr[:, :, :], ACT.Copy).then_inc(s_av, 1)
                if not back:
                    weights_high(11)
                if back:
                    deviation("w2", 2, b)
                if front:
                    deviation("wo", 1, c)

            all_chunks(act, front_back)

        @block.vector
        def _(dve):
            chain = {"n": 0}

            def link(ins):
                chain["n"] += 1
                ins.then_inc(s_chain, 1)
                dve.wait_ge(s_chain, chain["n"])

            def weights_low(n):
                dve.wait_ge(s_whi, n + 1)
                nc.vector.scalar_tensor_tensor(pieces[n][3], pieces[n][0], W_SCALE, pieces[n][2], ALU.mult, ALU.subtract)\
                    .then_inc(s_wlo, 1)

            def low_of_tr(dst, high_done, count, done):
                dve.wait_ge(high_done, count)
                nc.vector.tensor_tensor(dst[:, 1, :, :], tr[:, :, :], dst[:, 0, :, :], ALU.subtract).then_inc(done, 1)

            weights_low(0)
            weights_low(1)
            dve.wait_ge(s_small, 5 * 16)
            link(nc.vector.memset(eps[:, :], EPS))
            link(nc.vector.tensor_scalar(tmp[:, 2, :], theta[:, :], 1.0 / TWO_PI, ROUND, ALU.mult, ALU.add))
            link(nc.vector.tensor_scalar(tmp[:, 2, :], tmp[:, 2, :], ROUND, None, ALU.subtract))
            link(nc.vector.scalar_tensor_tensor(theta[:, :], tmp[:, 2, :], -6.28125, theta[:, :], ALU.mult, ALU.add))
            link(nc.vector.scalar_tensor_tensor(theta[:, :], tmp[:, 2, :], -(TWO_PI - 6.28125), theta[:, :], ALU.mult, ALU.add))
            link(nc.vector.tensor_scalar(turns[:, :], theta[:, :], 1.0 / TWO_PI, None, ALU.mult))
            link(nc.vector.tensor_scalar(tmp[:, 0, :], turns[:, :], 0.25, None, ALU.add))
            link(nc.vector.tensor_copy(tmp[:, 1, :], turns[:, :]))
            for i in range(2):
                link(nc.vector.tensor_scalar(tmp[:, 2, :], tmp[:, i, :], ROUND, ROUND, ALU.add, ALU.subtract))
                last = nc.vector.tensor_tensor(tmp[:, i, :], tmp[:, i, :], tmp[:, 2, :], ALU.subtract)
                if i == 0:
                    link(last)
            last.then_inc(s_parv, 1)
            link(nc.vector.tensor_scalar(b_q[:, :], b_q[:, :], DK ** -0.5, None, ALU.mult))
            link(nc.vector.scalar_tensor_tensor(turns[:, :], b_1[:, :], 0.1 / TWO_PI, turns[:, :], ALU.mult, ALU.add))
            dve.wait_ge(s_par, 1)
            link(nc.vector.tensor_tensor(tmp[:, 0, :], tmp[:, 0, :], w_re[:, :], ALU.mult))
            link(nc.vector.tensor_tensor(tmp[:, 1, :], tmp[:, 1, :], w_im[:, :], ALU.mult))
            link(nc.vector.tensor_tensor(tmp[:, 0, :], tmp[:, 0, :], tmp[:, 1, :], ALU.add))
            link(nc.vector.tensor_scalar(tmp[:, 0, :], tmp[:, 0, :], 0.1, None, ALU.mult))
            nc.vector.tensor_tensor(gain[:, :], tmp[:, 0, :], w_im[:, :], ALU.mult).then_inc(s_parv, 1)
            dve.wait_ge(s_parv, 2)
            weights_low(2)
            weights_low(3)

            def residual(n, c, x, xb_sem, into, tiles=range(NT)):
                for t in tiles:
                    dve.wait_ge(s_nat[n], c * NT + t + 1)
                    if t == 0:
                        dve.wait_ge(xb_sem, c + 1)
                    nc.vector.scalar_tensor_tensor(into[:, t, :], nat[:, t, :], UNSCALE, x[:, t, :], ALU.mult, ALU.add)\
                        .then_inc(s_r[n], 1)

            def statistics(n, i, c, x):
                for t in range(NT):
                    dve.wait_ge(s_r[n], c * NT + t + 1)
                    nc.vector.bn_stats(stats[:, i, t, :], x[:, t, :]).then_inc(s_st[n], 1)
                dve.wait_ge(s_st[n], (c + 1) * NT)
                dve.sem_inc(s_tick, 1)
                for t in range(NT):
                    last = nc.vector.bn_aggr(mv[:, i, t, :], stats[:, i, t, :])
                last.then_inc(s_mv[n], 1)

            def normalize(n, i, c, x):
                dve.wait_ge(s_sd[n], c + 1)
                nc.vector.reciprocal(rstd[:, i, :], std[:, i, :]).then_inc(s_rs[n], 1)
                dve.wait_ge(s_rs[n], c + 1)
                for t in range(NT):
                    nc.vector.tensor_scalar(x[:, t, :], x[:, t, :], mv[:, i, t, 0:1], rstd[:, i, t:t + 1],
                                            ALU.subtract, ALU.mult).then_inc(s_x[n], 1)

            def whole_turns(b, n):
                dve.wait_ge(s_h, b * NU + n + 1)
                nc.vector.tensor_scalar(whole[:, n % 2, :, :], arg[:, n % 3, :, :], ROUND, ROUND, ALU.add, ALU.subtract)\
                    .then_inc(s_wh, 1)

            def mix(b, n):
                dve.wait_ge(s_sin, b * NU + n + 1)
                for i in range(2):
                    f = 2 * n + i
                    nc.vector.scalar_tensor_tensor(hid[:, n % 3, i, :], arg[:, n % 3, i, :], gain[:, f:f + 1],
                                                   hid[:, n % 3, i, :], ALU.mult, ALU.add).then_inc(s_mix, 1)

            def act_low(b, n):
                dve.wait_ge(s_act, b * NU + n + 1)
                nc.vector.scalar_tensor_tensor(act16[:, 1, 2 * n:2 * n + 2, :], hid[:, n % 3, :, :], 0.0,
                                               act16[:, 0, 2 * n:2 * n + 2, :], ALU.max, ALU.subtract).then_inc(s_actl, 1)

            def unit(b, n):
                if n < NU:
                    whole_turns(b, n)
                if 0 < n <= NU:
                    mix(b, n - 1)
                if n > 1:
                    act_low(b, n - 2)

            def mask(c):
                dve.wait_ge(s_mask, (c + 1) * 16)
                nc.vector.tensor_scalar(keep[:, :, :], mask_i[:, :, :], 0.0, None, ALU.not_equal).then_inc(s_keep, 1)
                dve.wait_ge(s_keep, c * 2 + 1)
                nc.vector.tensor_scalar(fill[:, :, :], keep[:, :, :], 1.0, MASKED, ALU.subtract, ALU.mult).then_inc(s_keep, 1)

            def masked(c, t, lanes):
                for lane in lanes:
                    unit = t * LANES + lane
                    dve.wait_ge(s_scp, c * 8 + unit + 1)
                    if lane == 0:
                        dve.wait_ge(s_keep, c * 2 + 2)
                    nc.vector.tensor_tensor(pr[:, t, HU * lane:HU * (lane + 1), :],
                                            sps[:, unit % 2, 0:HU * CTX].rearrange("p (h k) -> p h k", k=CTX),
                                            keep[:, t:t + 1, :].broadcast_to([P, HU, CTX]), ALU.mult).then_inc(s_sc, 1)

            def softmax_a(c, t):
                base = (c * NT + t) * 3
                dve.wait_ge(s_sc, c * 8 + (t + 1) * LANES)
                nc.vector.tensor_tensor(pr[:, t, :, :], pr[:, t, :, :], fill[:, t:t + 1, :].broadcast_to([P, HEADS, CTX]),
                                        ALU.add).then_inc(s_sma, 1)
                dve.wait_ge(s_sma, base + 1)
                nc.vector.tensor_reduce(smax[:, t, :], pr[:, t, :, :], AXIS_X, ALU.max).then_inc(s_sma, 1)
                dve.wait_ge(s_sma, base + 2)
                nc.vector.tensor_tensor(pr[:, t, :, :], pr[:, t, :, :],
                                        smax[:, t, :].unsqueeze(2).broadcast_to([P, HEADS, CTX]), ALU.subtract)\
                    .then_inc(s_sma, 1)

            def softmax_b(c, t):
                dve.wait_ge(s_pexp, c * NT + t + 1)
                nc.vector.tensor_reduce(ssum[:, t, :], pr[:, t, :, :], AXIS_X, ALU.add).then_inc(s_ss, 1)
                dve.wait_ge(s_ss, c * NT + t + 1)
                nc.vector.reciprocal(sinv[:, t, :], ssum[:, t, :]).then_inc(s_smb, 1)


            def front_back(c, batch, front, back):
                b = c - 1
                if front:
                    mask(c)
                    residual("outproj", c, x_in, s_xb["xin"], x1, range(1))
                if back:
                    low_of_tr(x2_16, s_x2t, c, s_x2l)
                if front:
                    residual("outproj", c, x_in, s_xb["xin"], x1, range(1, NT))
                    statistics("outproj", 0, c, x1)
                    normalize("outproj", 0, c, x1)
                if not back:
                    weights_low(4)
                    weights_low(5)
                if back:
                    for n in range(4):
                        unit(b, n)
                if front:
                    low_of_tr(xa16, s_x1t, c + 1, s_x1l)
                if back:
                    for n in range(4, 7):
                        unit(b, n)
                if not back:
                    weights_low(6)
                    weights_low(7)
                if front:
                    masked(c, 0, (0, 1))
                if back:
                    unit(b, 7)
                if front:
                    masked(c, 0, (2, 3))
                if back:
                    unit(b, 8)
                if front:
                    softmax_a(c, 0)
                    masked(c, 1, (0, 1))
                if back:
                    unit(b, 9)
                if front:
                    masked(c, 1, (2, 3))
                    softmax_b(c, 0)
                    softmax_a(c, 1)
                if not back:
                    weights_low(8)
                if front:
                    softmax_b(c, 1)
                if not back:
                    weights_low(9)
                if not back:
                    weights_low(10)
                if back:
                    dve.wait_ge(s_out, b * 16)
                    residual("w2", b, x2, s_xb["wo"], x3, range(1))
                if front:
                    low_of_tr(xa16, s_av, c + 1, s_avl)
                if back:
                    residual("w2", b, x2, s_xb["wo"], x3, range(1, NT))
                    statistics("w2", 2, b, x3)
                    normalize("w2", 2, b, x3)
                if not back:
                    weights_low(11)
                if front:
                    residual("wo", c, x1, s_xb["outproj"], x2)
                    statistics("wo", 1, c, x2)
                    normalize("wo", 1, c, x2)

            all_chunks(dve, front_back)

        @block.gpsimd
        def _(pool):
            def add_bias(x, row, done):
                nc.gpsimd.tensor_tensor(x[:, :, :], x[:, :, :], rows[:, row:row + 1, :].broadcast_to([P, NT, D]), ALU.add)\
                    .then_inc(done, 1)

            def bias_x_in(c):
                pool.wait_ge(s_xin, (c + 1) * 16)
                add_bias(x_in, 0, s_xb["xin"])

            def fraction(b, n):
                pool.wait_ge(s_wh, b * NU + n + 1)
                nc.gpsimd.tensor_tensor(arg[:, n % 3, :, :], arg[:, n % 3, :, :], whole[:, n % 2, :, :], ALU.subtract)\
                    .then_inc(s_fr, 1)

            def probs(c, t):
                pool.wait_ge(s_smb, c * NT + t + 1)
                nc.gpsimd.tensor_tensor(pr[:, t, :, :], pr[:, t, :, :],
                                        sinv[:, t, :].unsqueeze(2).broadcast_to([P, HEADS, CTX]), ALU.mult).then_inc(s_pn, 1)

            def y_low(c):
                pool.wait_ge(s_yh, c + 1)
                nc.gpsimd.tensor_tensor(y16[:, 1, :, :], y_t[:, :, :], y16[:, 0, :, :], ALU.subtract).then_inc(s_yl, 1)

            y_low(0)
            pool.wait_ge(s_rows, 3 * 16)
            bias_x_in(0)

            def front_back(c, batch, front, back):
                b = c - 1
                if back:
                    pool.wait_ge(s_x2tp, c)
                    add_bias(x2, 2, s_xb["wo"])
                if back:
                    for n in range(5):
                        fraction(b, n)
                if front:
                    pool.wait_ge(s_x1tp, c + 1)
                    add_bias(x1, 1, s_xb["outproj"])
                if back:
                    for n in range(5, 8):
                        fraction(b, n)
                if front:
                    if not (isinstance(c, int) and c == CHUNKS - 1):
                        y_low(c + 1)
                    for t in range(NT):
                        probs(c, t)
                    if not (isinstance(c, int) and c == CHUNKS - 1):
                        bias_x_in(c + 1)

            all_chunks(pool, front_back)


def program(nc, a):
    with ExitStack() as ctx:
        def sb(name, shape, dt=FP32):
            return ctx.enter_context(nc.sbuf_tensor(name, shape, dt))

        region = sb("region", [P, 8 * 2 * 2048], FP16)
        parts = [region[:, n * 4096:(n + 1) * 4096].bitcast(FP32) for n in range(8)]
        wk, wv = (parts[n].rearrange("p (k n) -> p k n", k=KD) for n in range(2))
        ctx_t = parts[6][:, 0:KD * BATCH * CTX].rearrange("p (k b t) -> p k b t", k=KD, b=BATCH)
        k_t = parts[6][:, 1024:1024 + BATCH * KD * CTX].rearrange("p (b k t) -> p b k t", b=BATCH, k=KD)
        b_v, ones, b_k = parts[7][0:1, 0:D], parts[7][0:1, D:D + CTX], parts[7][:, 2 * D - KD:2 * D]
        v = parts[7][0:CTX, 1024:1024 + BATCH * D].rearrange("p (b n) -> p b n", b=BATCH)

        def rows_of(name, k0=0):
            return a[name].rearrange("(k p) n -> p k n", p=P)[:, k0:k0 + 4, :]

        a = dict(
            a, region=region, k_t=k_t, v=v, b_k=b_k,
            ident=sb("ident", [P, P]),
            s_ident=ctx.enter_context(nc.semaphore("identity_ready")),
            s_early=ctx.enter_context(nc.semaphore("early_weights_loaded")),
            kv_inputs=(ctx_t, wk, wv, b_v, ones),
            kv_loads=((ctx_t, a["ctx_t"].rearrange("(k p) b t -> p k b t", p=P)), (wk, rows_of("wk_t")),
                      (wv, rows_of("wv_t")), (b_v, a["b_v"]), (b_k, a["b_k"])),
            early_pieces=[(parts[2 + n].rearrange("p (k n) -> p k n", k=4), src, None, None) for n, src in enumerate(
                (rows_of("w_out"), rows_of("w_out", 4), rows_of("wq_t"), rows_of("wo_t")))],
            w_1_split=region[:, 0:4 * 4096].rearrange("p (s k n) -> p s k n", s=2, k=KD),
            w_2_split=region[:, 4 * 4096:8 * 4096].rearrange("p (s k n) -> p s k n", s=2, k=NF),
        )
        selective_scan_phase(nc, a)
        attention_ffn_phase(nc, a)


def kernel(**inputs):
    import numpy as np
    import concourse.bacc as bacc
    from concourse.bass_utils import run_bass_kernel_spmd

    def arr(name):
        return np.asarray(inputs[name])

    def columns(v):
        return np.ascontiguousarray(v.reshape(-1, P).T)

    x = arr("x").reshape(TOKENS, D)
    arrays = {
        "x": x,
        "x_t": x.T,
        "mask": arr("mask_1x1xSxS2_ik0")[0, 0],
        "ctx_t": arr("ctx_1024").transpose(2, 0, 1),
        "w_in": arr("L0_attn_W_in"), "b_in": columns(arr("L0_attn_b_in")),
        "w_xproj": arr("L0_attn_W_xproj"), "b_xproj": arr("L0_attn_b_xproj").reshape(-1, 1),
        "w_dt": arr("L0_attn_W_dt"), "b_dt": columns(arr("L0_attn_b_dt")),
        "a_log": arr("L0_attn_A_log"), "d_param": columns(arr("L0_attn_D_param")),
        "w_out": arr("L0_attn_W_out"), "b_out": arr("L0_attn_b_out").reshape(1, -1),
        "wq_t": arr("L0_xattn_wq_w").T, "wk_t": arr("L0_xattn_wk_w").T,
        "wv_t": arr("L0_xattn_wv_w").T, "wo_t": arr("L0_xattn_wo_w").T,
        "b_q": columns(arr("L0_xattn_wq_b")), "b_k": columns(arr("L0_xattn_wk_b")),
        "b_v": arr("L0_xattn_wv_b").reshape(1, -1), "b_o": arr("L0_xattn_wo_b").reshape(1, -1),
        "w_1": arr("L0_ffn_W1"), "b_1": columns(arr("L0_ffn_b1")),
        "theta": columns(arr("L0_ffn_quantum_phases")),
        "w_re": columns(arr("L0_ffn_quantum_weights_real")), "w_im": columns(arr("L0_ffn_quantum_weights_imag")),
        "w_2": arr("L0_ffn_W2"), "b_2": arr("L0_ffn_b2").reshape(1, -1),
    }
    nc = bacc.Bacc("TRN2", target_bir_lowering=False, num_devices=1)
    aps, sent = {}, {}
    for name, value in arrays.items():
        sent[f"dram_{name}"] = np.ascontiguousarray(value)
        aps[name] = nc.dram_tensor(f"dram_{name}", value.shape, mybir.dt.from_np(value.dtype), kind="ExternalInput").ap()
    aps["bc"] = nc.dram_tensor("bc_dram", (CHUNKS, 2 * NSTATE, TC), FP32, kind="Internal").ap()
    aps["y_t"] = nc.dram_tensor("y_t_dram", (INNER, TOKENS), FP32, kind="Internal").ap()
    aps["out"] = nc.dram_tensor("result", (TOKENS, D), FP32, kind="ExternalOutput").ap()
    program(nc, aps)
    r = run_bass_kernel_spmd(nc, [sent], core_ids=[0])
    return r.results[0]["result"].reshape(BATCH, SEQ, D)
```
